# Optimizing a Trainium2 kernel written in Bass

```python
import numpy as np
import jax
import jax.numpy as jnp

def _softmax(x, axis=-1):
    return jax.nn.softmax(x, axis=axis)
def _gelu(x):
    return jax.nn.gelu(x, approximate=True)
def _silu(x):
    return jax.nn.silu(x)
def _sigmoid(x):
    return jax.nn.sigmoid(x)
def _layernorm(x, axis=-1, eps=1e-5):
    m = jnp.mean(x, axis=axis, keepdims=True)
    v = jnp.var(x, axis=axis, keepdims=True)
    return (x - m) / jnp.sqrt(v + eps)
def _scatter_add(tgt, idx, src, axis=0):
    return tgt.at[idx].add(src)
def _segment_sum(src, seg, n):
    return jax.ops.segment_sum(src, seg, n)

kernel_name = 'mk_conv_preact_d1_conv_nchw512_abde29'

def setup_inputs(seed: int = 0):
    np.random.seed(seed)
    _w = jnp.asarray
    def _rec_inputs():
        import jax
        import jax.numpy as jnp
        _gk = jax.random.key(seed)
        x = -8.268e-05 + 0.9999 * jax.random.normal(jax.random.fold_in(_gk, 1), (32, 512, 56, 56), jnp.float32)
        return x
    x = _rec_inputs()
    def _L0_conv_setup():
        import jax, jax.numpy as jnp
        import numpy as np
        B, C, H, W = (32, 512, 56, 56)
        key = jax.random.key(seed)
        k1, k2, k3 = jax.random.split(key, 3)
        x = jax.random.normal(k1, (B, C, H, W), dtype=jnp.float32)
        scale = 1.0 / np.sqrt(C)
        W1 = jax.random.normal(k2, (C, C), dtype=jnp.float32) * scale
        W3 = jax.random.normal(k3, (C, C), dtype=jnp.float32) * scale
        return {'x': x, 'W1': W1, 'W3': W3}
    _L0_conv_all = _L0_conv_setup()
    _L0_conv_in = {k: v for k, v in _L0_conv_all.items() if k in ('W1', 'W3', )}
    del _L0_conv_all

    return {
        "x": x,
        "L0_conv_W1": _L0_conv_in["W1"],
        "L0_conv_W3": _L0_conv_in["W3"],
    }

def reference(x, L0_conv_W1, L0_conv_W3):
    import jax
    import jax.numpy as jnp
    def _L0_conv_ref(x, W1, W3):
        import jax, jax.numpy as jnp
        import numpy as np
        B, C, H, W = (32, 512, 56, 56)
        x = jax.nn.relu(x)
        avg_region = jnp.mean(x, axis=(2, 3), keepdims=True)
        peak_region = jnp.max(x, axis=(2, 3), keepdims=True)
        x = jnp.where(peak_region - avg_region < 0.5, 0.0, x)
        cmax = jnp.max(x, axis=1, keepdims=True)
        cmean = jnp.mean(x, axis=1, keepdims=True)
        bb = 1.0 - jnp.exp(-jnp.abs(cmax - cmean))
        x = bb * x
        x_max = jnp.max(x, axis=(2, 3), keepdims=True)
        pooled = jnp.mean(x, axis=(2, 3))
        control1 = jax.nn.sigmoid(pooled @ W1.T)[:, :, None, None]
        control3 = jax.nn.relu(pooled @ W3.T)
        control3 = jnp.where(control3 < 1.0, 1.2, control3)[:, :, None, None]
        thres = control1 * control3 * x_max
        return jnp.where(x < thres, 0.0, x)

    def _gn(v, G=32, eps=1e-5):
        B_, C_, H_, W_ = v.shape
        g = v.reshape(B_, G, C_ // G, H_, W_)
        m = jnp.mean(g, axis=(2, 3, 4), keepdims=True)
        s = jnp.var(g, axis=(2, 3, 4), keepdims=True)
        return ((g - m) / jnp.sqrt(s + eps)).reshape(v.shape)

    def _ln_c(v, eps=1e-6):
        m = jnp.mean(v, axis=1, keepdims=True)
        s = jnp.var(v, axis=1, keepdims=True)
        return (v - m) / jnp.sqrt(s + eps)

    def _ln_t(v, eps=1e-5):
        m = jnp.mean(v, axis=-1, keepdims=True)
        s = jnp.var(v, axis=-1, keepdims=True)
        return (v - m) / jnp.sqrt(s + eps)

    def _to_tokens(v):
        B_, C_, H_, W_ = v.shape
        return v.reshape(B_, C_, H_ * W_).transpose(0, 2, 1)
    def _from_tokens(t, like):
        B_, C_, H_, W_ = like.shape
        return t.transpose(0, 2, 1).reshape(B_, C_, H_, W_)

    x = x + _L0_conv_ref(_gn(x), L0_conv_W1, L0_conv_W3)
    return x


_drawn_inputs = setup_inputs


def setup_inputs(seed=0):
    import zlib

    import numpy as np

    out = dict(_drawn_inputs(seed))
    spreads = {}
    factors = {'L0_conv_W3': 7.162}
    for name, (base, spread) in spreads.items():
        noise = np.random.default_rng([zlib.crc32(name.encode()), seed]).standard_normal(out[name].shape)
        drawn = base * np.exp(spread * noise) if base else spread * noise
        out[name] = jnp.asarray(drawn.astype(out[name].dtype))
    for name, factor in factors.items():
        out[name] = (out[name] * factor).astype(out[name].dtype)
    return out
```

```python
from contextlib import ExitStack

import concourse.bass as bass
from concourse import mybir

F32 = mybir.dt.float32
I32 = mybir.dt.int32
ALU = mybir.AluOpType
ACT = mybir.ActivationFunctionType
AX = mybir.AxisListType

P = 128
GROUPS = 32
GN_EPS = 1e-5
PEAK_MARGIN = 0.5
CONTROL_FLOOR = 1.0
CONTROL_DEFAULT = 1.2

CHUNK = 392
BLOCK = 98
SUBSET = 128
BN_CHUNK = 448

SHARED = 2


class Sample:

    def __init__(self, i, parity):
        self.i, self.parity = i, parity

    def count(self, per_sample, upto):
        return self.i * (2 * per_sample) + (self.parity * per_sample + upto)

    def slot_count(self, upto):
        return self.i * 16 + 16 * upto

    def next(self):
        return Sample(self.i, 1) if self.parity == 0 else Sample(self.i + 1, 0)


class Steps:

    def __init__(self, eng, sem, sample, per_sample):
        self.eng, self.sem, self.sample, self.per_sample = eng, sem, sample, per_sample
        self.done = 0

    def step(self, ins):
        self.done += 1
        ins.then_inc(self.sem, 1)

    def wait(self, back=0):
        self.eng.wait_ge(self.sem, self.sample.count(self.per_sample, self.done - back))


def gated_sparsifier(nc, x, w1, w3, out):
    B, C, H, W = x.shape
    HW = H * W
    T = C // P
    TA = T - SHARED
    Q = HW // CHUNK
    J = CHUNK // BLOCK
    NBLK = Q * J
    BANKS = Q // 4
    NG = 4
    GC = Q // NG
    GPIX = GC * CHUNK
    HALF = HW // 2
    NBN = HW // BN_CHUNK
    PER_GROUP = C // GROUPS
    assert T == 4 and Q == 8 and HW == Q * CHUNK and CHUNK == J * BLOCK and B % 2 == 0
    assert NBN * BN_CHUNK == HW

    x_tiles = x.rearrange("b (t p) h w -> b p t (h w)", p=P)
    out_tiles = out.rearrange("b (t p) h w -> b p t (h w)", p=P)

    with ExitStack() as ctx:
        def sb(name, shape, dt=F32):
            return ctx.enter_context(nc.sbuf_tensor(name, shape, dt))

        def ps(name, shape):
            return ctx.enter_context(nc.psum_tensor(name, shape, F32))

        def sem(name):
            return ctx.enter_context(nc.semaphore(name))

        xs = sb("xs", [P, 2, T, HW])
        rs = sb("rs", [P, SHARED + 2 * TA, HW])
        mx = sb("mx", [P, HW])
        wt = sb("wt", [P, 2, T, C])
        ident = sb("ident", [P, P])
        group_avg = sb("group_avg", [P, P])
        chan_avg = sb("chan_avg", [P, 32])
        ones = sb("ones", [P, 1])
        row_pick = sb("row_pick", [P, 4])
        cmean_rows = sb("cmean_rows", [P, BANKS, CHUNK])
        half_neg = sb("half_neg", [P, T])
        bnst = sb("bnst", [P, SHARED, NBN, 6])
        bnag = sb("bnag", [P, SHARED, 2])
        bnsq = sb("bnsq", [P, SHARED])
        st = sb("st", [P, 2, T])
        gst = sb("gst", [P, 2, T])
        gsq = sb("gsq", [P, T])
        gvar = sb("gvar", [P, T])
        geps = sb("geps", [P, T])
        rstd = sb("rstd", [P, T])
        mrs = sb("mrs", [P, T])
        shift = sb("shift", [P, T])
        rsum = sb("rsum", [P, T])
        peak = sb("peak", [P, T])
        margin = sb("margin", [P, T])
        least = sb("least", [P, 1])
        fails = sb("fails", [P, 1])
        flag = sb("flag", [1, 1], I32)
        fpeak = sb("fpeak", [P, T])
        fmargin = sb("fmargin", [P, T])
        keep = sb("keep", [P, T])
        cmax = sb("cmax", [P, NBLK])
        diff = sb("diff", [P, NBLK])
        negdiff = sb("negdiff", [P, NBLK])
        expd = sb("expd", [P, NBLK])
        bb = sb("bb", [P, NBLK])
        ymax_parts = sb("ymax_parts", [P, T, NG])
        ymax = sb("ymax", [P, T])
        pooled = sb("pooled", [P, T, 2])
        logits = sb("logits", [P, 2 * T])
        exp_neg = sb("exp_neg", [P, T])
        den = sb("den", [P, T])
        control1 = sb("control1", [P, T])
        c3_high = sb("c3_high", [P, T])
        c3_low = sb("c3_low", [P, T])
        control3 = sb("control3", [P, T])
        control = sb("control", [P, T])
        thres = sb("thres", [P, T])

        ps_pix = ps("ps_pix", [P, 4, 512])
        ps_rows = ps("ps_rows", [P, BANKS, 512])
        ps_small = ps("ps_small", [P, 512])
        ps_group = ps("ps_group", [P, 512])
        ps_cols = ps_small[0:BLOCK, 0:NBLK]
        ps_control = ps_small[:, 64:64 + 4 * T].rearrange("p (m h) -> p m h", h=2)
        ps_count = ps_small[0:1, 128:129]

        x_loaded = [[sem(f"x_loaded_{p}_{t}") for t in range(T)] for p in range(2)]
        x_stored = [[sem(f"x_stored_{p}_{t}") for t in range(T)] for p in range(2)]
        w_loaded = [sem("w1_loaded"), sem("w3_loaded")]
        settled = {e: sem(f"settled_{n}") for n, e in
                   (("pe", nc.tensor), ("dve", nc.vector), ("pool", nc.gpsimd))}
        const_step = sem("const_step")
        const_step_pool = sem("const_step_pool")
        mrs_ready = sem("mrs_ready")
        consts_ready = sem("consts_ready")
        ones_ready = sem("ones_ready")
        w_turned = sem("w_turned")
        wt_ready = sem("wt_ready")
        act_step = sem("act_step")
        stats_act = sem("stats_act")
        stats_dve = sem("stats_dve")
        group_sums = sem("group_sums")
        group_copied = sem("group_copied")
        pool_step = sem("pool_step")
        affine_ready = sem("affine_ready")
        relu_done = sem("relu_done")
        fails_ready = sem("fails_ready")
        count_ready = sem("count_ready")
        flag_ready = sem("flag_ready")
        mask_step = sem("mask_step")
        r_final = sem("r_final")
        rows_tried = sem("rows_tried")
        rows_final = sem("rows_final")
        rows_copied = sem("rows_copied")
        cols_ready = sem("cols_ready")
        max_half = sem("max_half")
        turned = sem("turned")
        cmax_part = sem("cmax_part")
        negdiff_ready = sem("negdiff_ready")
        expd_ready = sem("expd_ready")
        bb_ready = sem("bb_ready")
        bb_rows = sem("bb_rows")
        gated = sem("gated")
        pooled_ready = sem("pooled_ready")
        control_ready = sem("control_ready")
        logits_ready = sem("logits_ready")
        exp_neg_ready = sem("exp_neg_ready")
        dve_step = sem("dve_step")
        kept = sem("kept")
        added_dve = sem("added_dve")
        added_pool = sem("added_pool")

        def slot(parity, t):
            return t if t < SHARED else SHARED + TA * parity + (t - SHARED)

        def r_tile(s, t):
            return rs[:, slot(s.parity, t), :]

        DVE_CREDIT = SHARED
        POOL_CREDIT = 2 * TA

        def wait_r_slot_free(eng, s, t):
            if t < SHARED:
                eng.wait_ge(added_dve, s.count(SHARED, t + 1))
            else:
                eng.wait_ge(added_pool, s.count(TA, t - SHARED + 1))

        def wait_added(eng, s, t):
            if t < SHARED:
                eng.wait_ge(added_dve, s.count(SHARED, t + 1 + DVE_CREDIT))
            else:
                eng.wait_ge(added_pool, s.count(TA, t - SHARED + 1 + POOL_CREDIT))

        def wait_loaded(eng, s, t):
            eng.wait_ge(x_loaded[s.parity][t], s.slot_count(1))

        def each_sample(eng, body):
            with eng.Fori(0, B // 2 - 1) as i:
                for parity in range(2):
                    body(Sample(i, parity), True, True)
            for parity in range(2):
                body(Sample(B // 2 - 1, parity), parity == 0, False)

        def settle(eng):
            eng.sem_inc(settled[eng], 1)

        block = ctx.enter_context(nc.Block())

        @block.sync
        def _(sp):
            def load(s, t):
                sp.dma_start(xs[:, s.parity, t, :], x_tiles[bass.ds(s.i * 2 + s.parity, 1), :, t, :]
                             .rearrange("b p f -> (b p) f")).then_inc(x_loaded[s.parity][t], 16)

            def store(s, t):
                wait_added(sp, s, t)
                sp.dma_start(out_tiles[bass.ds(s.i * 2 + s.parity, 1), :, t, :]
                             .rearrange("b p f -> (b p) f"), xs[:, s.parity, t, :]
                             ).then_inc(x_stored[s.parity][t], 16)

            for t in range(T):
                load(Sample(0, 0), t)
            for m, w in enumerate((w1, w3)):
                sp.dma_start(rs[:, slot(1, SHARED + m), 0:T * C].rearrange("p (k c) -> p k c", k=T),
                             w.rearrange("(k p) c -> p k c", p=P)).then_inc(w_loaded[m], 16)
            for t in range(T):
                load(Sample(0, 1), t)

            def reload(s, t):
                sp.wait_ge(x_stored[s.parity][t], s.slot_count(1))
                load(Sample(s.i + 1, s.parity), t)

            def sample(s, _, has_second_next):
                for t in range(T):
                    store(s, t)
                    if has_second_next and t >= 1:
                        reload(s, t - 1)
                if has_second_next:
                    reload(s, T - 1)

            each_sample(sp, sample)
            for parity in range(2):
                for t in range(T):
                    sp.wait_ge(x_stored[parity][t], 16 * (B // 2))

        @block.tensor
        def _(pe):
            def channel_mean_tile(s, t, last_sem):
                for q in range(Q):
                    b, k = q // 4, q % 4
                    mm = pe.matmul(ps_rows[32 * k:32 * k + 32, b, 0:CHUNK], chan_avg[:, :],
                                   r_tile(s, t)[:, CHUNK * q:CHUNK * (q + 1)],
                                   start=(t == SHARED), stop=(t == SHARED - 1), skip_group_check=True,
                                   tile_position=(0, 32 * k))
                if last_sem is not None:
                    mm.then_inc(last_sem, 1)

            order = [2, 3, 0, 1]

            def group_stats(s):
                pe.wait_ge(stats_act, s.count(1, 1))
                pe.wait_ge(stats_dve, s.count(1, 1))
                pe.matmul(ps_group[:, 0:2 * T], group_avg[:, :], st[:, :, :].rearrange("p a t -> p (a t)"),
                          start=True, stop=True).then_inc(group_sums, 1)

            def channel_mean_first(s):
                for n, t in enumerate(order[:-1]):
                    pe.wait_ge(relu_done, s.count(T, n + 1))
                    channel_mean_tile(s, t, None)

            pe.wait_ge(consts_ready, 1)
            pe.wait_ge(ones_ready, 1)
            for m in range(2):
                pe.wait_ge(w_loaded[m], 16)
                for k in range(T):
                    n = T * m + k
                    if n >= 4:
                        pe.wait_ge(wt_ready, n - 3)
                    for c in range(T):
                        mm = pe.transpose(ps_pix[:, n % 4, P * c:P * (c + 1)],
                                          rs[:, slot(1, SHARED + m), C * c + P * k:C * c + P * (k + 1)],
                                          ident[:, :])
                    mm.then_inc(w_turned, 1)
            group_stats(Sample(0, 0))
            channel_mean_first(Sample(0, 0))

            def sample(s, has_next, _):
                pe.wait_ge(fails_ready, s.count(1, 1))
                pe.matmul(ps_count, fails[:, :], ones[:, :], start=True, stop=True).then_inc(count_ready, 1)
                channel_mean_tile(s, order[-1], rows_tried)
                pe.wait_ge(flag_ready, s.count(1, 1))
                settle(pe)
                open_channels = pe.value_load(flag[0:1, 0:1], min_val=0, max_val=P)
                with pe.If(open_channels > 0):
                    pe.wait_ge(r_final, s.count(1, 1))
                    for n, t in enumerate(order):
                        channel_mean_tile(s, t, rows_final if n == T - 1 else None)
                with pe.Else():
                    pe.sem_inc(rows_final, 1)

                for part in range(4):
                    if part % 2 == 0:
                        pe.wait_ge(max_half, s.count(2, part // 2 + 1))
                    if part >= 2:
                        pe.wait_ge(cmax_part, s.count(4, part - 1))
                    for n in range(8):
                        blk = 8 * part + n
                        mm = pe.transpose(ps_pix[0:BLOCK, 2 * (part % 2) + n // 4, P * (n % 4):P * (n % 4 + 1)],
                                          mx[:, BLOCK * blk:BLOCK * (blk + 1)], ident[:, :])
                    mm.then_inc(turned, 1)

                pe.wait_ge(rows_copied, s.count(1, 1))
                for b in range(BANKS):
                    for j in range(J):
                        first = 4 * J * b + j
                        mm = pe.matmul(ps_cols[:, first:first + 3 * J + 1:J],
                                       cmean_rows[:, b, BLOCK * j:BLOCK * (j + 1)], row_pick[:, :],
                                       start=True, stop=True)
                mm.then_inc(cols_ready, 1)

                pe.wait_ge(bb_ready, s.count(1, 1))
                for g in range(NG):
                    if g >= 2:
                        pe.wait_ge(gated, s.count(NG * T, T * (g - 1)))
                    for n in range(GC * J):
                        blk = GC * J * g + n
                        mm = pe.matmul(ps_pix[:, 2 * (g % 2) + n // J, BLOCK * (n % J):BLOCK * (n % J + 1)],
                                       bb[0:BLOCK, blk:blk + 1].to_broadcast([BLOCK, P]),
                                       ident[0:BLOCK, 0:BLOCK], start=True, stop=True)
                    mm.then_inc(bb_rows, 1)

                for k in range(T):
                    pe.wait_ge(pooled_ready, s.count(T, k + 1))
                    for m in range(2):
                        for c in range(T):
                            mm = pe.matmul(ps_control[:, T * m + c, :], wt[:, m, k, P * c:P * (c + 1)],
                                           pooled[:, k, :], start=(k == 0 and m == 0 and c == 0),
                                           stop=(k == T - 1), skip_group_check=True)
                mm.then_inc(control_ready, 1)

                if has_next:
                    group_stats(s.next())
                    channel_mean_first(s.next())

            each_sample(pe, sample)

        @block.scalar
        def _(act):
            def stats(s):
                steps = Steps(act, act_step, s, TA)
                for t in range(SHARED, T):
                    wait_loaded(act, s, t)
                    wait_r_slot_free(act, s, t)
                    steps.step(act.activation(r_tile(s, t), xs[:, s.parity, t, :], ACT.Square,
                                              scale=float(HW) ** -0.5, accum_out=st[:, 1, t:t + 1]))
                for t in range(SHARED, T):
                    steps.wait(back=T - 1 - t)
                    last = act.activation(r_tile(s, t), xs[:, s.parity, t, :], ACT.Identity,
                                          scale=1.0 / HW, accum_out=st[:, 0, t:t + 1])
                last.then_inc(stats_act, 1)

            def copy_group(s):
                act.wait_ge(group_sums, s.count(1, 1))
                act.activation(gst[:, :, :].rearrange("p a t -> p (a t)"), ps_group[:, 0:2 * T],
                               ACT.Identity).then_inc(group_copied, 1)

            def relu(s):
                act.wait_ge(affine_ready, s.count(1, 1))
                for t in [2, 3, 0, 1]:
                    if t < SHARED:
                        wait_r_slot_free(act, s, t)
                    act.activation(r_tile(s, t), xs[:, s.parity, t, :], ACT.Relu, bias=shift[:, t:t + 1],
                                   scale=rstd[:, t:t + 1], accum_out=rsum[:, t:t + 1]).then_inc(relu_done, 1)

            stats(Sample(0, 0))
            copy_group(Sample(0, 0))
            relu(Sample(0, 0))
            act.wait_ge(wt_ready, 2 * T)

            def sample(s, has_next, _):
                if has_next:
                    stats(s.next())
                act.wait_ge(rows_tried, s.count(1, 1))
                act.wait_ge(rows_final, s.count(1, 1))
                act.activation(cmean_rows[:, :, :], ps_rows[:, :, 0:CHUNK], ACT.Identity).then_inc(rows_copied, 1)
                act.wait_ge(negdiff_ready, s.count(1, 1))
                act.activation(expd[0:BLOCK, :], negdiff[0:BLOCK, :], ACT.Exp).then_inc(expd_ready, 1)
                for h in range(2):
                    for t in range(T):
                        act.wait_ge(gated, s.count(NG * T, T * (2 * h + 1) + t + 1))
                        y = r_tile(s, t)[:, HALF * h:HALF * (h + 1)]
                        ins = act.activation(y, y, ACT.Identity, scale=1.0, accum_out=pooled[:, t, h:h + 1])
                        if h == 1:
                            ins.then_inc(pooled_ready, 1)
                act.wait_ge(logits_ready, s.count(1, 1))
                act.activation(exp_neg[:, :], logits[:, 0:T], ACT.Exp, scale=-1.0).then_inc(exp_neg_ready, 1)
                if has_next:
                    copy_group(s.next())
                    relu(s.next())

            each_sample(act, sample)

        @block.vector
        def _(dve):
            MASK_STEPS = 4
            DVE_STEPS = 21

            dve.memset(chan_avg[:, :], 1.0 / C)
            dve.memset(half_neg[:, :], -0.5)
            dve.memset(ones[:, :], 1.0).then_inc(ones_ready, 1)

            def bn_chunks(s, t, chunks):
                for c in chunks:
                    ins = dve.bn_stats(bnst[:, t, c, :], xs[:, s.parity, t, BN_CHUNK * c:BN_CHUNK * (c + 1)])
                return ins

            def stats_part(s, n):
                per = SHARED * NBN
                cut = [0, 3, 8, per]
                for u in range(cut[n], cut[n + 1]):
                    if u % NBN == 0:
                        wait_loaded(dve, s, u // NBN)
                    ins = bn_chunks(s, u // NBN, [u % NBN])
                return ins

            def stats_close(s, steps, ins):
                steps.step(ins)
                steps.wait()
                settle(dve)
                for t in range(SHARED):
                    ins = dve.bn_aggr(bnag[:, t, :], bnst[:, t, :, :].rearrange("p c s -> p (c s)"))
                steps.step(ins)
                steps.wait()
                dve.tensor_copy(st[:, 0, 0:SHARED], bnag[:, :, 0])
                steps.step(dve.tensor_tensor(bnsq[:, :], bnag[:, :, 0], bnag[:, :, 0], ALU.mult))
                steps.wait()
                dve.tensor_tensor(st[:, 1, 0:SHARED], bnsq[:, :], bnag[:, :, 1], ALU.add).then_inc(stats_dve, 1)

            first = Sample(0, 0)
            steps = Steps(dve, const_step, first, 0)
            for n in range(3):
                ins = stats_part(first, n)
            stats_close(first, steps, ins)
            for n in range(2 * T):
                dve.wait_ge(w_turned, n + 1)
                dve.tensor_copy(wt[:, n // T, n % T, :], ps_pix[:, n % 4, :]).then_inc(wt_ready, 1)
            dve.sem_inc(added_dve, DVE_CREDIT)

            def mask_channels(s):
                masks = Steps(dve, mask_step, s, MASK_STEPS)
                dve.wait_ge(rows_tried, s.count(1, 1))
                for t in range(T):
                    ins = dve.tensor_reduce(fpeak[:, t:t + 1], r_tile(s, t), AX.X, ALU.max)
                masks.step(ins)
                masks.wait()
                masks.step(dve.scalar_tensor_tensor(fmargin[:, :], rsum[:, :], -1.0 / HW, fpeak[:, :],
                                                    ALU.mult, ALU.add))
                masks.wait()
                masks.step(dve.tensor_scalar(keep[:, :], fmargin[:, :], PEAK_MARGIN, None, ALU.is_ge))
                masks.wait()
                for t in range(T):
                    ins = dve.tensor_scalar(r_tile(s, t), r_tile(s, t), keep[:, t:t + 1], None, ALU.mult)
                masks.step(ins)
                masks.wait()
                assert masks.done == MASK_STEPS

            def sample(s, has_next, _):
                steps = Steps(dve, dve_step, s, DVE_STEPS)
                nxt = s.next() if has_next else None

                dve.wait_ge(relu_done, s.count(T, T))
                a = slot(s.parity, SHARED)
                dve.tensor_reduce(peak[:, 0:SHARED], rs[:, 0:SHARED, 0:SUBSET], AX.X, ALU.max)
                steps.step(dve.tensor_reduce(peak[:, SHARED:T], rs[:, a:a + TA, 0:SUBSET], AX.X, ALU.max))
                steps.wait()
                steps.step(dve.scalar_tensor_tensor(margin[:, :], rsum[:, :], -1.0 / HW, peak[:, :],
                                                    ALU.mult, ALU.add))
                steps.wait()
                steps.step(dve.tensor_reduce(least[:, :], margin[:, :], AX.X, ALU.min))
                steps.wait()
                dve.tensor_scalar(fails[:, :], least[:, :], PEAK_MARGIN, None, ALU.is_lt
                                  ).then_inc(fails_ready, 1)
                if has_next:
                    stats_part(nxt, 0)
                dve.wait_ge(count_ready, s.count(1, 1))
                dve.tensor_copy(flag[:, :], ps_count).then_inc(flag_ready, 1)
                dve.wait_ge(flag_ready, s.count(1, 1))
                settle(dve)
                open_channels = dve.value_load(flag[0:1, 0:1], min_val=0, max_val=P)
                with dve.If(open_channels > 0):
                    mask_channels(s)
                    dve.sem_inc(r_final, 1)
                with dve.Else():
                    dve.sem_inc(mask_step, MASK_STEPS)
                    dve.sem_inc(r_final, 1)

                for n, t in enumerate(range(1, T)):
                    for h in range(2):
                        cols = slice(HALF * h, HALF * (h + 1))
                        prev = r_tile(s, 0) if n == 0 else mx[:, :]
                        if n > 0:
                            steps.wait(back=0 if n == T - 2 and h == 1 else 1)
                        ins = dve.tensor_tensor(mx[:, cols], prev[:, cols], r_tile(s, t)[:, cols], ALU.max)
                        if t == T - 1:
                            ins.then_inc(max_half, 1)
                        else:
                            steps.step(ins)
                for part in range(4):
                    dve.wait_ge(turned, s.count(4, part + 1))
                    b = 2 * (part % 2)
                    ins = dve.tensor_reduce(
                        cmax[0:BLOCK, 8 * part:8 * (part + 1)],
                        ps_pix[0:BLOCK, b:b + 2, :].rearrange("p b (n c) -> p (b n) c", c=P), AX.X, ALU.max)
                    ins.then_inc(cmax_part, 1)
                dve.wait_ge(cmax_part, s.count(4, 4))
                dve.wait_ge(cols_ready, s.count(1, 1))
                steps.step(dve.tensor_tensor(diff[0:BLOCK, :], cmax[0:BLOCK, :], ps_cols, ALU.subtract))
                steps.wait()
                dve.scalar_tensor_tensor(negdiff[0:BLOCK, :], diff[0:BLOCK, :], -1.0, diff[0:BLOCK, :],
                                         ALU.mult, ALU.min).then_inc(negdiff_ready, 1)
                if has_next:
                    stats_part(nxt, 1)
                dve.wait_ge(expd_ready, s.count(1, 1))
                dve.tensor_scalar(bb[0:BLOCK, :], expd[0:BLOCK, :], -1.0, 1.0, ALU.mult, ALU.add
                                  ).then_inc(bb_ready, 1)

                for g in range(NG):
                    dve.wait_ge(bb_rows, s.count(NG, g + 1))
                    settle(dve)
                    b = 2 * (g % 2)
                    for t in range(T):
                        y = r_tile(s, t)[:, GPIX * g:GPIX * (g + 1)].rearrange("p (b f) -> p b f", f=CHUNK)
                        dve.tensor_tensor_reduce(out=y, in0=y, in1=ps_pix[:, b:b + 2, 0:CHUNK], scale=1.0,
                                                 scalar=0.0, op0=ALU.mult, op1=ALU.max,
                                                 accum_out=ymax_parts[:, t, g:g + 1]).then_inc(gated, 1)
                if has_next:
                    stats_close(nxt, steps, stats_part(nxt, 2))
                else:
                    dve.sem_inc(dve_step, 3)
                    steps.done += 3

                dve.wait_ge(gated, s.count(NG * T, NG * T))
                steps.step(dve.tensor_reduce(ymax[:, :], ymax_parts[:, :, :], AX.X, ALU.max))
                dve.wait_ge(control_ready, s.count(1, 1))
                steps.step(dve.tensor_reduce(control1[:, :], ps_control[:, 0:T, :], AX.X, ALU.add))
                steps.step(dve.tensor_reduce(control3[:, :], ps_control[:, T:2 * T, :], AX.X, ALU.add))
                steps.wait(back=1)
                dve.tensor_scalar(logits[:, 0:T], control1[:, :], 1.0 / HW, None, ALU.mult
                                  ).then_inc(logits_ready, 1)
                steps.wait()
                steps.step(dve.tensor_scalar(logits[:, T:2 * T], control3[:, :], 1.0 / HW, None, ALU.mult))
                steps.wait()
                dve.scalar_tensor_tensor(c3_high[:, :], logits[:, T:2 * T], CONTROL_FLOOR,
                                         logits[:, T:2 * T], ALU.is_ge, ALU.mult)
                steps.step(dve.tensor_scalar(c3_low[:, :], logits[:, T:2 * T], CONTROL_FLOOR, CONTROL_DEFAULT,
                                             ALU.is_lt, ALU.mult))
                steps.wait()
                steps.step(dve.tensor_tensor(control3[:, :], c3_high[:, :], c3_low[:, :], ALU.add))
                dve.wait_ge(exp_neg_ready, s.count(1, 1))
                steps.step(dve.tensor_scalar(den[:, :], exp_neg[:, :], 1.0, None, ALU.add))
                steps.wait()
                steps.step(dve.reciprocal(control1[:, :], den[:, :]))
                steps.wait()
                steps.step(dve.tensor_tensor(control[:, :], control1[:, :], control3[:, :], ALU.mult))
                steps.wait()
                steps.step(dve.tensor_tensor(thres[:, :], control[:, :], ymax[:, :], ALU.mult))
                steps.wait()

                def keep_tile(t):
                    r = r_tile(s, t)
                    return dve.scalar_tensor_tensor(r, r, thres[:, t:t + 1], r, ALU.is_ge, ALU.mult
                                                    ).then_inc(kept, 1)

                def add_tile(t):
                    xt = xs[:, s.parity, t, :]
                    dve.wait_ge(kept, s.count(T, t + 1))
                    dve.tensor_tensor(xt, xt, r_tile(s, t), ALU.add).then_inc(added_dve, 1)

                keep_tile(0)
                keep_tile(1)
                add_tile(0)
                add_tile(1)
                keep_tile(2)
                keep_tile(3)
                assert steps.done == DVE_STEPS, steps.done

            each_sample(dve, sample)

        @block.gpsimd
        def _(pool):
            POOL_STEPS = 4
            pool.memset(ident[:, :], 0.0)
            pool.memset(row_pick[:, :], 0.0)
            pool.memset(group_avg[:, :], 1.0 / PER_GROUP).then_inc(const_step_pool, 1)
            pool.wait_ge(const_step_pool, 1)
            pool.affine_select(out=ident[:, :], in_=ident[:, :], compare_op=ALU.not_equal, fill=1.0, base=0,
                               pattern=[[-1, P]], channel_multiplier=1)
            pool.affine_select(out=row_pick[:, :], in_=row_pick[:, :], compare_op=ALU.not_equal, fill=1.0,
                               base=0, pattern=[[-32, 4]], channel_multiplier=1)
            blocks = group_avg[:, :].rearrange("p (g c) -> p g c", c=PER_GROUP)
            pool.affine_select(out=blocks, in_=blocks, compare_op=ALU.is_ge, fill=0.0, base=0,
                               pattern=[[-PER_GROUP, P // PER_GROUP], [0, PER_GROUP]], channel_multiplier=1
                               ).then_inc(const_step_pool, 1)
            pool.wait_ge(const_step_pool, 2)
            pool.affine_select(out=blocks, in_=blocks, compare_op=ALU.is_ge, fill=0.0, base=PER_GROUP - 1,
                               pattern=[[PER_GROUP, P // PER_GROUP], [0, PER_GROUP]], channel_multiplier=-1
                               ).then_inc(consts_ready, 1)
            pool.sem_inc(added_pool, POOL_CREDIT)
            pool.wait_ge(ones_ready, 1)

            def affine(s):
                steps = Steps(pool, pool_step, s, POOL_STEPS)
                pool.wait_ge(group_copied, s.count(1, 1))
                steps.step(pool.tensor_tensor(gsq[:, :], gst[:, 0, :], gst[:, 0, :], ALU.mult))
                steps.wait()
                steps.step(pool.tensor_tensor(gvar[:, :], gst[:, 1, :], gsq[:, :], ALU.subtract))
                steps.wait()
                settle(pool)
                steps.step(pool.tensor_scalar(geps[:, :], gvar[:, :], 0.0, GN_EPS, ALU.max, ALU.add))
                steps.wait()
                pool.tensor_tensor(rstd[:, :], geps[:, :], half_neg[:, :], ALU.pow).then_inc(pool_step, 1)
                steps.done += 1
                steps.wait()
                pool.tensor_tensor(mrs[:, :], gst[:, 0, :], rstd[:, :], ALU.mult).then_inc(mrs_ready, 1)
                pool.wait_ge(mrs_ready, s.count(1, 1))
                settle(pool)
                pool.tensor_scalar(shift[:, :], mrs[:, :], -1.0, 1.0, ALU.mult, ALU.mult
                                   ).then_inc(affine_ready, 1)
                assert steps.done == POOL_STEPS

            affine(Sample(0, 0))

            def sample(s, has_next, _):
                if has_next:
                    affine(s.next())
                for t in range(SHARED, T):
                    pool.wait_ge(kept, s.count(T, t + 1))
                    xt = xs[:, s.parity, t, :]
                    pool.tensor_tensor(xt, xt, r_tile(s, t), ALU.add).then_inc(added_pool, 1)

            each_sample(pool, sample)


_INS = ["x", "L0_conv_W1", "L0_conv_W3"]


def kernel(**inputs):
    import numpy as np
    import concourse.bacc as bacc
    from concourse.bass_utils import run_bass_kernel_spmd

    nc = bacc.Bacc("TRN2", target_bir_lowering=False, num_devices=1)
    arrays, args = {}, []
    for name in _INS:
        a = np.ascontiguousarray(inputs[name])
        arrays[f"in_{name}"] = a
        args.append(nc.dram_tensor(f"in_{name}", a.shape, mybir.dt.from_np(a.dtype), kind="ExternalInput").ap())
    shape = inputs["x"].shape
    args.append(nc.dram_tensor("out_0", shape, F32, kind="ExternalOutput").ap())
    gated_sparsifier(nc, *args)
    r = run_bass_kernel_spmd(nc, [arrays], core_ids=[0])
    return r.results[0]["out_0"]
```

```python
from contextlib import ExitStack

import concourse.bass as bass
from concourse import mybir

F32 = mybir.dt.float32
BF16 = mybir.dt.bfloat16
I32 = mybir.dt.int32
ALU = mybir.AluOpType
ACT = mybir.ActivationFunctionType
AX = mybir.AxisListType

P = 128
GROUPS = 32
GN_EPS = 1e-5
PEAK_MARGIN = 0.5
CONTROL_FLOOR = 1.0
CONTROL_DEFAULT = 1.2

CHUNK = 392
BLOCK = 98
SUBSET = 128
BN_CHUNK = 448

SHARED = 1


class Sample:

    def __init__(self, i, parity):
        self.i, self.parity = i, parity

    def count(self, per_sample, upto):
        return self.i * (2 * per_sample) + (self.parity * per_sample + upto)

    def slot_count(self, upto):
        return self.i * 16 + 16 * upto

    def next(self):
        return Sample(self.i, 1) if self.parity == 0 else Sample(self.i + 1, 0)


class Steps:

    def __init__(self, eng, sem, sample, per_sample):
        self.eng, self.sem, self.sample, self.per_sample = eng, sem, sample, per_sample
        self.done = 0

    def step(self, ins):
        self.done += 1
        ins.then_inc(self.sem, 1)

    def wait(self, back=0):
        self.eng.wait_ge(self.sem, self.sample.count(self.per_sample, self.done - back))


def gated_sparsifier(nc, x, w1, w3, out):
    B, C, H, W = x.shape
    HW = H * W
    T = C // P
    TA = T - SHARED
    Q = HW // CHUNK
    J = CHUNK // BLOCK
    NBLK = Q * J
    BANKS = Q // 4
    NG = 4
    GC = Q // NG
    GPIX = GC * CHUNK
    POOLED_GROUPS = [(g, g + 1) for g in range(NG)]
    NPOOL = len(POOLED_GROUPS)
    HALF = HW // 2
    NBN = HW // BN_CHUNK
    PER_GROUP = C // GROUPS
    assert T == 4 and Q == 8 and HW == Q * CHUNK and CHUNK == J * BLOCK and B % 2 == 0
    assert NBN * BN_CHUNK == HW

    x_tiles = x.rearrange("b (t p) h w -> b p t (h w)", p=P)
    out_tiles = out.rearrange("b (t p) h w -> b p t (h w)", p=P)

    with ExitStack() as ctx:
        def sb(name, shape, dt=F32):
            return ctx.enter_context(nc.sbuf_tensor(name, shape, dt))

        def ps(name, shape):
            return ctx.enter_context(nc.psum_tensor(name, shape, F32))

        def sem(name):
            return ctx.enter_context(nc.semaphore(name))

        xs = sb("xs", [P, 2, T, HW])
        rs = sb("rs", [P, SHARED + 2 * TA, HW])
        mx = sb("mx", [P, HW])
        wt = sb("wt", [P, 2, T, C])
        ident = sb("ident", [P, P])
        group_avg = sb("group_avg", [P, P])
        chan_avg = sb("chan_avg", [P, 32])
        ones = sb("ones", [P, 1])
        row_pick = sb("row_pick", [P, 4])
        part_pick = sb("part_pick", [P, 2])
        ident_bf = sb("ident_bf", [P, P], BF16)
        cmean_rows = sb("cmean_rows", [P, BANKS, CHUNK])
        control_sb = cmean_rows[0:64, :, :].rearrange("p b f -> p (b f)")[:, 0:C]
        half_neg = sb("half_neg", [P, T])
        bnst = sb("bnst", [P, 2, NBN, 6])
        bnag = sb("bnag", [P, 2, 2])
        bnsq = sb("bnsq", [P, 2])
        st = sb("st", [P, 2, T])
        gst = sb("gst", [P, 2, T])
        gsq = sb("gsq", [P, T])
        gvar = sb("gvar", [P, T])
        geps = sb("geps", [P, T])
        rstd = sb("rstd", [P, T])
        mrs = sb("mrs", [P, T])
        shift = sb("shift", [P, T])
        rsum = sb("rsum", [P, T])
        peak = sb("peak", [P, T])
        margin = sb("margin", [P, T])
        least = sb("least", [P, 1])
        fails = sb("fails", [P, 1])
        flag = sb("flag", [1, 1], I32)
        fpeak = sb("fpeak", [P, T])
        fmargin = sb("fmargin", [P, T])
        keep = sb("keep", [P, T])
        cmax = sb("cmax", [P, NBLK])
        diff = sb("diff", [P, NBLK])
        negdiff = sb("negdiff", [P, NBLK])
        expd = sb("expd", [P, NBLK])
        bb = sb("bb", [P, NBLK])
        bb_rest = sb("bb_rest", [P, NBLK])
        bb_parts = sb("bb_parts", [P, 3, NBLK], BF16)
        ymax_parts = sb("ymax_parts", [P, T, NG])
        ymax = sb("ymax", [P, T])
        pooled = sb("pooled", [P, T, NPOOL])
        logits = sb("logits", [P, 2 * T])
        exp_neg = sb("exp_neg", [P, T])
        den = sb("den", [P, T])
        control1 = sb("control1", [P, T])
        c3_high = sb("c3_high", [P, T])
        c3_low = sb("c3_low", [P, T])
        control3 = sb("control3", [P, T])
        control = sb("control", [P, T])
        thres = sb("thres", [P, T])

        ps_pix = ps("ps_pix", [P, 4, 512])
        ps_rows = ps("ps_rows", [P, BANKS, 512])
        ps_small = ps("ps_small", [P, 512])
        ps_group = ps("ps_group", [P, 512])
        ps_cols = ps_small[0:BLOCK, 0:NBLK]
        ps_control = ps_small[:, 64:64 + 2 * T].rearrange("p (m t) -> p m t", t=T)
        ps_count = ps_small[0:1, 128:129]

        def turn_banks(part):
            first = 2 * [0, 1, None, 0][part] if part != 2 else None
            return ps_rows[:, :, :] if part == 2 else ps_pix[:, first:first + 2, :]

        x_loaded = [[sem(f"x_loaded_{p}_{t}") for t in range(T)] for p in range(2)]
        x_stored = [[sem(f"x_stored_{p}_{t}") for t in range(T)] for p in range(2)]
        w_loaded = [sem("w1_loaded"), sem("w3_loaded")]
        settled = {e: sem(f"settled_{n}") for n, e in
                   (("pe", nc.tensor), ("dve", nc.vector), ("pool", nc.gpsimd), ("sp", nc.sync))}
        const_step = sem("const_step")
        const_step_pool = sem("const_step_pool")
        mrs_ready = sem("mrs_ready")
        consts_ready = sem("consts_ready")
        ones_ready = sem("ones_ready")
        w_turned = sem("w_turned")
        wt_ready = sem("wt_ready")
        act_step = sem("act_step")
        stats_act = sem("stats_act")
        stats_dve = sem("stats_dve")
        group_sums = sem("group_sums")
        group_copied = sem("group_copied")
        pool_step = sem("pool_step")
        affine_ready = sem("affine_ready")
        relu_done = sem("relu_done")
        fails_ready = sem("fails_ready")
        count_ready = sem("count_ready")
        flag_ready = sem("flag_ready")
        mask_step = sem("mask_step")
        r_final = sem("r_final")
        rows_tried = sem("rows_tried")
        rows_final = sem("rows_final")
        rows_copied = sem("rows_copied")
        cols_ready = sem("cols_ready")
        max_part = sem("max_part")
        turned = sem("turned")
        cmax_part = sem("cmax_part")
        negdiff_ready = sem("negdiff_ready")
        expd_ready = sem("expd_ready")
        bb_ready = sem("bb_ready")
        bb_rows = sem("bb_rows")
        gated = sem("gated")
        pooled_ready = sem("pooled_ready")
        control_rows = sem("control_rows")
        control_copied = sem("control_copied")
        control_ready = sem("control_ready")
        logits_ready = sem("logits_ready")
        exp_neg_ready = sem("exp_neg_ready")
        dve_step = sem("dve_step")
        kept = sem("kept")
        added_dve = sem("added_dve")
        added_pool = sem("added_pool")

        def slot(parity, t):
            return t if t < SHARED else SHARED + TA * parity + (t - SHARED)

        def r_tile(s, t):
            return rs[:, slot(s.parity, t), :]

        DVE_CREDIT = 1
        POOL_CREDIT = 2 * (T - 1)

        def wait_r_slot_free(eng, s, t):
            if t == 0:
                eng.wait_ge(added_dve, s.count(1, 1))
            else:
                eng.wait_ge(added_pool, s.count(T - 1, t))

        def wait_added(eng, s, t):
            if t == 0:
                eng.wait_ge(added_dve, s.count(1, 1 + DVE_CREDIT))
            else:
                eng.wait_ge(added_pool, s.count(T - 1, t + POOL_CREDIT))

        ADD_ORDER = [0, 1, 2, 3]
        STATS_DVE = [1, 2]
        STATS_ACT = [0, 3]
        RELU_ORDER = [1, 2, 3, 0]

        def wait_loaded(eng, s, t):
            eng.wait_ge(x_loaded[s.parity][t], s.slot_count(1))

        def each_sample(eng, body):
            with eng.Fori(0, B // 2 - 1) as i:
                for parity in range(2):
                    body(Sample(i, parity), True, True)
            for parity in range(2):
                body(Sample(B // 2 - 1, parity), parity == 0, False)

        def settle(eng):
            eng.sem_inc(settled[eng], 1)

        block = ctx.enter_context(nc.Block())

        @block.sync
        def _(sp):
            def load(s, t):
                sp.dma_start(xs[:, s.parity, t, :], x_tiles[bass.ds(s.i * 2 + s.parity, 1), :, t, :]
                             .rearrange("b p f -> (b p) f")).then_inc(x_loaded[s.parity][t], 16)

            def store(s, t):
                wait_added(sp, s, t)
                settle(sp)
                sp.dma_start(out_tiles[bass.ds(s.i * 2 + s.parity, 1), :, t, :]
                             .rearrange("b p f -> (b p) f"), xs[:, s.parity, t, :]
                             ).then_inc(x_stored[s.parity][t], 16)

            for t in range(T):
                load(Sample(0, 0), t)
            for m, w in enumerate((w1, w3)):
                sp.dma_start(rs[:, slot(1, SHARED + m), 0:T * C].rearrange("p (k c) -> p k c", k=T),
                             w.rearrange("(k p) c -> p k c", p=P)).then_inc(w_loaded[m], 16)
            for t in range(T):
                load(Sample(0, 1), t)

            def reload(s, t):
                sp.wait_ge(x_stored[s.parity][t], s.slot_count(1))
                settle(sp)
                load(Sample(s.i + 1, s.parity), t)

            def sample(s, _, has_second_next):
                for n, t in enumerate(ADD_ORDER):
                    store(s, t)
                    if has_second_next and n >= 1:
                        reload(s, ADD_ORDER[n - 1])
                if has_second_next:
                    reload(s, ADD_ORDER[-1])

            each_sample(sp, sample)
            for parity in range(2):
                for t in range(T):
                    sp.wait_ge(x_stored[parity][t], 16 * (B // 2))

        @block.tensor
        def _(pe):
            def channel_mean_tile(s, t, last_sem):
                for q in range(Q):
                    b, k = q // 4, q % 4
                    mm = pe.matmul(ps_rows[32 * k:32 * k + 32, b, 0:CHUNK], chan_avg[:, :],
                                   r_tile(s, t)[:, CHUNK * q:CHUNK * (q + 1)],
                                   start=(t == RELU_ORDER[0]), stop=(t == RELU_ORDER[-1]), skip_group_check=True,
                                   tile_position=(0, 32 * k))
                if last_sem is not None:
                    mm.then_inc(last_sem, 1)

            order = RELU_ORDER

            def group_stats(s):
                pe.wait_ge(stats_act, s.count(1, 1))
                pe.wait_ge(stats_dve, s.count(1, 1))
                pe.matmul(ps_group[:, 0:2 * T], group_avg[:, :], st[:, :, :].rearrange("p a t -> p (a t)"),
                          start=True, stop=True).then_inc(group_sums, 1)

            def channel_mean_first(s):
                for n, t in enumerate(order[:-1]):
                    pe.wait_ge(relu_done, s.count(T, n + 1))
                    channel_mean_tile(s, t, None)

            pe.wait_ge(consts_ready, 1)
            pe.wait_ge(ones_ready, 1)
            for m in range(2):
                pe.wait_ge(w_loaded[m], 16)
                for k in range(T):
                    n = T * m + k
                    if n >= 4:
                        pe.wait_ge(wt_ready, n - 3)
                    for c in range(T):
                        mm = pe.transpose(ps_pix[:, n % 4, P * c:P * (c + 1)],
                                          rs[:, slot(1, SHARED + m), C * c + P * k:C * c + P * (k + 1)],
                                          ident[:, :])
                    mm.then_inc(w_turned, 1)
            group_stats(Sample(0, 0))
            channel_mean_first(Sample(0, 0))

            def sample(s, has_next, _):
                pe.wait_ge(fails_ready, s.count(1, 1))
                pe.matmul(ps_count, fails[:, :], ones[:, :], start=True, stop=True).then_inc(count_ready, 1)
                channel_mean_tile(s, order[-1], rows_tried)
                pe.wait_ge(flag_ready, s.count(1, 1))
                settle(pe)
                open_channels = pe.value_load(flag[0:1, 0:1], min_val=0, max_val=P)
                with pe.If(open_channels > 0):
                    pe.wait_ge(r_final, s.count(1, 1))
                    for n, t in enumerate(order):
                        channel_mean_tile(s, t, rows_final if n == T - 1 else None)
                with pe.Else():
                    pe.sem_inc(rows_final, 1)

                pe.wait_ge(rows_copied, s.count(1, 1))
                for b in range(BANKS):
                    for j in range(J):
                        first = 4 * J * b + j
                        mm = pe.matmul(ps_cols[:, first:first + 3 * J + 1:J],
                                       cmean_rows[:, b, BLOCK * j:BLOCK * (j + 1)], row_pick[:, :],
                                       start=True, stop=True)
                mm.then_inc(cols_ready, 1)

                for part in range(4):
                    pe.wait_ge(max_part, s.count(4, part + 1))
                    if part == 3:
                        pe.wait_ge(cmax_part, s.count(4, 1))
                    for n in range(8):
                        blk = 8 * part + n
                        mm = pe.transpose(turn_banks(part)[0:BLOCK, n // 4, P * (n % 4):P * (n % 4 + 1)],
                                          mx[:, BLOCK * blk:BLOCK * (blk + 1)], ident[:, :])
                    mm.then_inc(turned, 1)

                pe.wait_ge(bb_ready, s.count(1, 1))
                for g in range(NG):
                    if g >= 2:
                        pe.wait_ge(gated, s.count(NG * T, T * (g - 1)))
                    for n in range(GC * J):
                        blk = GC * J * g + n
                        for part in range(3):
                            mm = pe.matmul(ps_pix[:, 2 * (g % 2) + n // J, BLOCK * (n % J):BLOCK * (n % J + 1)],
                                           bb_parts[0:BLOCK, part, blk:blk + 1].to_broadcast([BLOCK, P]),
                                           ident_bf[0:BLOCK, 0:BLOCK], start=(part == 0), stop=(part == 2))
                    mm.then_inc(bb_rows, 1)

                for k in range(T):
                    pe.wait_ge(pooled_ready, s.count(T, k + 1))
                    for m in range(2):
                        mm = pe.matmul(ps_rows[32 * m:32 * m + NPOOL, 0, :], pooled[:, k, :], wt[:, m, k, :],
                                       start=(k == 0), stop=(k == T - 1), skip_group_check=True,
                                       tile_position=(0, 32 * m))
                mm.then_inc(control_rows, 1)
                pe.wait_ge(control_copied, s.count(1, 1))
                for c in range(T):
                    mm = pe.matmul(ps_control[:, :, c], control_sb[:, P * c:P * (c + 1)], part_pick[0:64, :],
                                   start=True, stop=True)
                mm.then_inc(control_ready, 1)

                if has_next:
                    group_stats(s.next())
                    channel_mean_first(s.next())

            each_sample(pe, sample)

        @block.scalar
        def _(act):
            def stats(s, t):
                steps = Steps(act, act_step, s, 3)
                steps.done = 2 * STATS_ACT.index(t)
                wait_loaded(act, s, t)
                idle = max(t, SHARED)
                wait_r_slot_free(act, s, idle)
                steps.step(act.activation(r_tile(s, idle), xs[:, s.parity, t, :], ACT.Square,
                                          scale=float(HW) ** -0.5, accum_out=st[:, 1, t:t + 1]))
                steps.wait()
                ins = act.activation(r_tile(s, idle), xs[:, s.parity, t, :], ACT.Identity,
                                     scale=1.0 / HW, accum_out=st[:, 0, t:t + 1])
                if t == STATS_ACT[-1]:
                    ins.then_inc(stats_act, 1)
                else:
                    steps.step(ins)

            def copy_group(s):
                act.wait_ge(group_sums, s.count(1, 1))
                act.activation(gst[:, :, :].rearrange("p a t -> p (a t)"), ps_group[:, 0:2 * T],
                               ACT.Identity).then_inc(group_copied, 1)

            def relu(s):
                act.wait_ge(affine_ready, s.count(1, 1))
                for t in RELU_ORDER:
                    if t != STATS_ACT[1]:
                        wait_r_slot_free(act, s, t)
                    act.activation(r_tile(s, t), xs[:, s.parity, t, :], ACT.Relu, bias=shift[:, t:t + 1],
                                   scale=rstd[:, t:t + 1], accum_out=rsum[:, t:t + 1]).then_inc(relu_done, 1)

            for t in STATS_ACT:
                stats(Sample(0, 0), t)
            copy_group(Sample(0, 0))
            relu(Sample(0, 0))
            act.wait_ge(wt_ready, 2 * T)

            def sample(s, has_next, _):
                act.wait_ge(rows_tried, s.count(1, 1))
                act.wait_ge(rows_final, s.count(1, 1))
                act.activation(cmean_rows[:, :, :], ps_rows[:, :, 0:CHUNK], ACT.Identity).then_inc(rows_copied, 1)
                if has_next:
                    stats(s.next(), STATS_ACT[0])
                act.wait_ge(negdiff_ready, s.count(1, 1))
                act.activation(expd[0:BLOCK, :], negdiff[0:BLOCK, :], ACT.Exp).then_inc(expd_ready, 1)
                for part, (g0, g1) in enumerate(POOLED_GROUPS):
                    for t in range(T):
                        act.wait_ge(gated, s.count(NG * T, T * (g1 - 1) + t + 1))
                        y = r_tile(s, t)[:, GPIX * g0:GPIX * g1]
                        ins = act.activation(y, y, ACT.Identity, accum_out=pooled[:, t, part:part + 1])
                        if part == NPOOL - 1:
                            ins.then_inc(pooled_ready, 1)
                act.wait_ge(control_rows, s.count(1, 1))
                act.activation(control_sb, ps_rows[0:64, 0, :], ACT.Identity).then_inc(control_copied, 1)
                act.wait_ge(logits_ready, s.count(1, 1))
                act.activation(exp_neg[:, :], logits[:, 0:T], ACT.Exp, scale=-1.0).then_inc(exp_neg_ready, 1)
                if has_next:
                    stats(s.next(), STATS_ACT[1])
                    copy_group(s.next())
                    relu(s.next())

            each_sample(act, sample)

        @block.vector
        def _(dve):
            MASK_STEPS = 7
            DVE_STEPS = 21

            dve.memset(chan_avg[:, :], 1.0 / C)
            dve.memset(ps_rows[0:64, 0, :], 0.0)
            dve.memset(half_neg[:, :], -0.5)
            dve.memset(ones[:, :], 1.0).then_inc(ones_ready, 1)

            def bn_chunks(s, t, chunks):
                for c in chunks:
                    ins = dve.bn_stats(bnst[:, t, c, :], xs[:, s.parity, STATS_DVE[t], BN_CHUNK * c:BN_CHUNK * (c + 1)])
                return ins

            def stats_part(s, n):
                per = 2 * NBN
                cut = [0, 1, 5, per]
                for u in range(cut[n], cut[n + 1]):
                    if u % NBN == 0:
                        wait_loaded(dve, s, STATS_DVE[u // NBN])
                    ins = bn_chunks(s, u // NBN, [u % NBN])
                return ins

            def stats_close(s, steps, ins):
                steps.step(ins)
                steps.wait()
                settle(dve)
                for t in range(2):
                    ins = dve.bn_aggr(bnag[:, t, :], bnst[:, t, :, :].rearrange("p c s -> p (c s)"))
                steps.step(ins)
                steps.wait()
                dve.tensor_copy(st[:, 0, 1:3], bnag[:, :, 0])
                steps.step(dve.tensor_tensor(bnsq[:, :], bnag[:, :, 0], bnag[:, :, 0], ALU.mult))
                steps.wait()
                dve.tensor_tensor(st[:, 1, 1:3], bnsq[:, :], bnag[:, :, 1], ALU.add).then_inc(stats_dve, 1)

            first = Sample(0, 0)
            steps = Steps(dve, const_step, first, 0)
            for n in range(3):
                ins = stats_part(first, n)
            stats_close(first, steps, ins)
            for n in range(2 * T):
                dve.wait_ge(w_turned, n + 1)
                dve.tensor_copy(wt[:, n // T, n % T, :], ps_pix[:, n % 4, :]).then_inc(wt_ready, 1)
            dve.sem_inc(added_dve, DVE_CREDIT)

            def mask_channels(s):
                masks = Steps(dve, mask_step, s, MASK_STEPS)
                dve.wait_ge(rows_tried, s.count(1, 1))
                for t in range(T):
                    ins = dve.tensor_reduce(fpeak[:, t:t + 1], r_tile(s, t), AX.X, ALU.max)
                masks.step(ins)
                masks.wait()
                masks.step(dve.scalar_tensor_tensor(fmargin[:, :], rsum[:, :], -1.0 / HW, fpeak[:, :],
                                                    ALU.mult, ALU.add))
                masks.wait()
                masks.step(dve.tensor_scalar(keep[:, :], fmargin[:, :], PEAK_MARGIN, None, ALU.is_ge))
                masks.wait()
                for t in range(T):
                    ins = dve.tensor_scalar(r_tile(s, t), r_tile(s, t), keep[:, t:t + 1], None, ALU.mult)
                masks.step(ins)
                masks.wait()
                return masks

            def sample(s, has_next, _):
                steps = Steps(dve, dve_step, s, DVE_STEPS)
                nxt = s.next() if has_next else None

                dve.wait_ge(relu_done, s.count(T, T))
                a = slot(s.parity, SHARED)
                dve.tensor_reduce(peak[:, 0:SHARED], rs[:, 0:SHARED, 0:SUBSET], AX.X, ALU.max)
                steps.step(dve.tensor_reduce(peak[:, SHARED:T], rs[:, a:a + TA, 0:SUBSET], AX.X, ALU.max))
                steps.wait()
                steps.step(dve.scalar_tensor_tensor(margin[:, :], rsum[:, :], -1.0 / HW, peak[:, :],
                                                    ALU.mult, ALU.add))
                steps.wait()
                steps.step(dve.tensor_reduce(least[:, :], margin[:, :], AX.X, ALU.min))
                steps.wait()
                dve.tensor_scalar(fails[:, :], least[:, :], PEAK_MARGIN, None, ALU.is_lt
                                  ).then_inc(fails_ready, 1)

                def max_step(n, h, after):
                    cols = slice(HALF * h, HALF * (h + 1))
                    prev = r_tile(s, 0) if n == 0 else mx[:, :]
                    if n > 0:
                        after.wait(back=1)
                    return dve.tensor_tensor(mx[:, cols], prev[:, cols], r_tile(s, n + 1)[:, cols], ALU.max)

                steps.step(max_step(0, 0, steps))
                dve.wait_ge(count_ready, s.count(1, 1))
                dve.tensor_copy(flag[:, :], ps_count).then_inc(flag_ready, 1)
                steps.step(max_step(0, 1, steps))
                steps.step(max_step(1, 0, steps))
                steps.step(max_step(1, 1, steps))
                dve.wait_ge(flag_ready, s.count(1, 1))
                settle(dve)
                open_channels = dve.value_load(flag[0:1, 0:1], min_val=0, max_val=P)
                with dve.If(open_channels > 0):
                    masks = mask_channels(s)
                    for n in range(2):
                        for h in range(2):
                            ins = max_step(n, h, masks)
                            if (n, h) == (1, 1):
                                ins.then_inc(r_final, 1)
                            else:
                                masks.step(ins)
                    assert masks.done == MASK_STEPS
                with dve.Else():
                    dve.sem_inc(mask_step, MASK_STEPS)
                    dve.sem_inc(r_final, 1)
                steps.wait()
                dve.wait_ge(r_final, s.count(1, 1))
                for part in range(4):
                    cols = slice(GPIX * part, GPIX * (part + 1))
                    dve.tensor_tensor(mx[:, cols], mx[:, cols], r_tile(s, T - 1)[:, cols], ALU.max
                                      ).then_inc(max_part, 1)
                for part in range(4):
                    dve.wait_ge(turned, s.count(4, part + 1))
                    ins = dve.tensor_reduce(
                        cmax[0:BLOCK, 8 * part:8 * (part + 1)],
                        turn_banks(part)[0:BLOCK, :, :].rearrange("p b (n c) -> p (b n) c", c=P), AX.X, ALU.max)
                    ins.then_inc(cmax_part, 1)
                dve.wait_ge(cmax_part, s.count(4, 4))
                dve.wait_ge(cols_ready, s.count(1, 1))
                steps.step(dve.tensor_tensor(diff[0:BLOCK, :], cmax[0:BLOCK, :], ps_cols, ALU.subtract))
                steps.wait()
                dve.scalar_tensor_tensor(negdiff[0:BLOCK, :], diff[0:BLOCK, :], -1.0, diff[0:BLOCK, :],
                                         ALU.mult, ALU.min).then_inc(negdiff_ready, 1)
                if has_next:
                    stats_part(nxt, 0)
                dve.wait_ge(expd_ready, s.count(1, 1))
                def cols_of(a):
                    return a[0:BLOCK, :]

                dve.tensor_scalar(cols_of(bb), cols_of(expd), -1.0, 1.0, ALU.mult, ALU.add)
                steps.step(dve.tensor_scalar(bb_parts[0:BLOCK, 0, :], cols_of(expd), -1.0, 1.0,
                                             ALU.mult, ALU.add))
                steps.wait()
                dve.tensor_tensor(cols_of(bb_rest), cols_of(bb), bb_parts[0:BLOCK, 0, :], ALU.subtract)
                steps.step(dve.tensor_tensor(bb_parts[0:BLOCK, 1, :], cols_of(bb), bb_parts[0:BLOCK, 0, :],
                                             ALU.subtract))
                steps.wait()
                dve.tensor_tensor(bb_parts[0:BLOCK, 2, :], cols_of(bb_rest), bb_parts[0:BLOCK, 1, :],
                                  ALU.subtract).then_inc(bb_ready, 1)
                if has_next:
                    stats_part(nxt, 1)

                for g in range(NG):
                    dve.wait_ge(bb_rows, s.count(NG, g + 1))
                    settle(dve)
                    b = 2 * (g % 2)
                    for t in range(T):
                        y = r_tile(s, t)[:, GPIX * g:GPIX * (g + 1)].rearrange("p (b f) -> p b f", f=CHUNK)
                        dve.tensor_tensor_reduce(out=y, in0=y, in1=ps_pix[:, b:b + 2, 0:CHUNK], scale=1.0,
                                                 scalar=0.0, op0=ALU.mult, op1=ALU.max,
                                                 accum_out=ymax_parts[:, t, g:g + 1]).then_inc(gated, 1)
                if has_next:
                    stats_close(nxt, steps, stats_part(nxt, 2))
                else:
                    dve.sem_inc(dve_step, 3)
                    steps.done += 3

                dve.wait_ge(gated, s.count(NG * T, NG * T))
                steps.step(dve.tensor_reduce(ymax[:, :], ymax_parts[:, :, :], AX.X, ALU.max))
                dve.wait_ge(control_ready, s.count(1, 1))
                dve.tensor_scalar(logits[:, 0:T], ps_control[:, 0, :], 1.0 / HW, None, ALU.mult
                                  ).then_inc(logits_ready, 1)
                steps.step(dve.tensor_scalar(logits[:, T:2 * T], ps_control[:, 1, :], 1.0 / HW, None, ALU.mult))
                steps.wait()
                dve.scalar_tensor_tensor(c3_high[:, :], logits[:, T:2 * T], CONTROL_FLOOR,
                                         logits[:, T:2 * T], ALU.is_ge, ALU.mult)
                steps.step(dve.tensor_scalar(c3_low[:, :], logits[:, T:2 * T], CONTROL_FLOOR, CONTROL_DEFAULT,
                                             ALU.is_lt, ALU.mult))
                steps.wait()
                steps.step(dve.tensor_tensor(control3[:, :], c3_high[:, :], c3_low[:, :], ALU.add))
                dve.wait_ge(exp_neg_ready, s.count(1, 1))
                steps.step(dve.tensor_scalar(den[:, :], exp_neg[:, :], 1.0, None, ALU.add))
                steps.wait()
                steps.step(dve.reciprocal(control1[:, :], den[:, :]))
                steps.wait()
                steps.step(dve.tensor_tensor(control[:, :], control1[:, :], control3[:, :], ALU.mult))
                steps.wait()
                steps.step(dve.tensor_tensor(thres[:, :], control[:, :], ymax[:, :], ALU.mult))
                steps.wait()

                def keep_tile(t):
                    r = r_tile(s, t)
                    return dve.scalar_tensor_tensor(r, r, thres[:, t:t + 1], r, ALU.is_ge, ALU.mult
                                                    ).then_inc(kept, 1)

                keep_tile(ADD_ORDER[0])
                keep_tile(ADD_ORDER[1])
                keep_tile(ADD_ORDER[2])
                xt = xs[:, s.parity, 0, :]
                dve.wait_ge(kept, s.count(T, 2))
                dve.tensor_tensor(xt, xt, r_tile(s, 0), ALU.add).then_inc(added_dve, 1)
                keep_tile(ADD_ORDER[3])
                assert steps.done == DVE_STEPS, steps.done

            each_sample(dve, sample)

        @block.gpsimd
        def _(pool):
            POOL_STEPS = 4
            pool.memset(ident[:, :], 0.0)
            pool.memset(row_pick[:, :], 0.0)
            pool.memset(part_pick[:, :], 0.0)
            pool.memset(group_avg[:, :], 1.0 / PER_GROUP).then_inc(const_step_pool, 1)
            pool.wait_ge(const_step_pool, 1)
            pool.affine_select(out=ident[:, :], in_=ident[:, :], compare_op=ALU.not_equal, fill=1.0, base=0,
                               pattern=[[-1, P]], channel_multiplier=1)
            pool.affine_select(out=row_pick[:, :], in_=row_pick[:, :], compare_op=ALU.not_equal, fill=1.0,
                               base=0, pattern=[[-32, 4]], channel_multiplier=1)
            blocks = group_avg[:, :].rearrange("p (g c) -> p g c", c=PER_GROUP)
            pool.affine_select(out=blocks, in_=blocks, compare_op=ALU.is_ge, fill=0.0, base=0,
                               pattern=[[-PER_GROUP, P // PER_GROUP], [0, PER_GROUP]], channel_multiplier=1
                               ).then_inc(const_step_pool, 1)
            pool.wait_ge(const_step_pool, 2)
            for n in range(NPOOL):
                pool.affine_select(out=part_pick[:, :], in_=part_pick[:, :], compare_op=ALU.not_equal, fill=1.0,
                                   base=-n, pattern=[[-32, 2]], channel_multiplier=1
                                   ).then_inc(const_step_pool, 1)
                pool.wait_ge(const_step_pool, 3 + n)
            pool.tensor_copy(ident_bf[:, :], ident[:, :])
            pool.affine_select(out=blocks, in_=blocks, compare_op=ALU.is_ge, fill=0.0, base=PER_GROUP - 1,
                               pattern=[[PER_GROUP, P // PER_GROUP], [0, PER_GROUP]], channel_multiplier=-1
                               ).then_inc(consts_ready, 1)
            pool.sem_inc(added_pool, POOL_CREDIT)
            pool.wait_ge(ones_ready, 1)

            def affine(s):
                steps = Steps(pool, pool_step, s, POOL_STEPS)
                pool.wait_ge(group_copied, s.count(1, 1))
                steps.step(pool.tensor_tensor(gsq[:, :], gst[:, 0, :], gst[:, 0, :], ALU.mult))
                steps.wait()
                steps.step(pool.tensor_tensor(gvar[:, :], gst[:, 1, :], gsq[:, :], ALU.subtract))
                steps.wait()
                settle(pool)
                steps.step(pool.tensor_scalar(geps[:, :], gvar[:, :], 0.0, GN_EPS, ALU.max, ALU.add))
                steps.wait()
                pool.tensor_tensor(rstd[:, :], geps[:, :], half_neg[:, :], ALU.pow).then_inc(pool_step, 1)
                steps.done += 1
                steps.wait()
                pool.tensor_tensor(mrs[:, :], gst[:, 0, :], rstd[:, :], ALU.mult).then_inc(mrs_ready, 1)
                pool.wait_ge(mrs_ready, s.count(1, 1))
                settle(pool)
                pool.tensor_scalar(shift[:, :], mrs[:, :], -1.0, 1.0, ALU.mult, ALU.mult
                                   ).then_inc(affine_ready, 1)
                assert steps.done == POOL_STEPS

            affine(Sample(0, 0))

            def sample(s, has_next, _):
                if has_next:
                    affine(s.next())
                for t in range(1, T):
                    pool.wait_ge(kept, s.count(T, ADD_ORDER.index(t) + 1))
                    xt = xs[:, s.parity, t, :]
                    pool.tensor_tensor(xt, xt, r_tile(s, t), ALU.add).then_inc(added_pool, 1)

            each_sample(pool, sample)


_INS = ["x", "L0_conv_W1", "L0_conv_W3"]


def kernel(**inputs):
    import numpy as np
    import concourse.bacc as bacc
    from concourse.bass_utils import run_bass_kernel_spmd

    nc = bacc.Bacc("TRN2", target_bir_lowering=False, num_devices=1, dynamic_dma_scratch_size=1024)
    arrays, args = {}, []
    for name in _INS:
        a = np.ascontiguousarray(inputs[name])
        arrays[f"in_{name}"] = a
        args.append(nc.dram_tensor(f"in_{name}", a.shape, mybir.dt.from_np(a.dtype), kind="ExternalInput").ap())
    shape = inputs["x"].shape
    args.append(nc.dram_tensor("out_0", shape, F32, kind="ExternalOutput").ap())
    gated_sparsifier(nc, *args)
    r = run_bass_kernel_spmd(nc, [arrays], core_ids=[0])
    return r.results[0]["out_0"]
```

```python
from contextlib import ExitStack

import concourse.bass as bass
from concourse import mybir

F32 = mybir.dt.float32
BF16 = mybir.dt.bfloat16
I32 = mybir.dt.int32
ALU = mybir.AluOpType
ACT = mybir.ActivationFunctionType
AX = mybir.AxisListType

P = 128
GROUPS = 32
GN_EPS = 1e-5
PEAK_MARGIN = 0.5
CONTROL_FLOOR = 1.0
CONTROL_DEFAULT = 1.2

CHUNK = 392
BLOCK = 98
SUBSET = 96
BN_CHUNK = 448

SHARED = 1
RELOADS_AFTER = [[], [0], [1], [2, 3], [], [4], [5], [6, 7]]


class Sample:

    def __init__(self, i, parity):
        self.i, self.parity = i, parity

    def count(self, per_sample, upto):
        return self.i * (2 * per_sample) + (self.parity * per_sample + upto)

    def slot_count(self, upto):
        return self.i * 16 + 16 * upto

    def next(self):
        return Sample(self.i, 1) if self.parity == 0 else Sample(self.i + 1, 0)


class Steps:

    def __init__(self, eng, sem, sample, per_sample):
        self.eng, self.sem, self.sample, self.per_sample = eng, sem, sample, per_sample
        self.done = 0

    def step(self, ins):
        self.done += 1
        ins.then_inc(self.sem, 1)

    def wait(self, back=0):
        self.eng.wait_ge(self.sem, self.sample.count(self.per_sample, self.done - back))


def gated_sparsifier(nc, x, w1, w3, out):
    B, C, H, W = x.shape
    HW = H * W
    T = C // P
    TA = T - SHARED
    Q = HW // CHUNK
    J = CHUNK // BLOCK
    NBLK = Q * J
    BANKS = Q // 4
    NG = 4
    GC = Q // NG
    GPIX = GC * CHUNK
    HALF = HW // 2
    NBN = HW // BN_CHUNK
    BN_CHUNKS = [4, 6]
    BN_PIXELS = [n * BN_CHUNK for n in BN_CHUNKS]
    PER_GROUP = C // GROUPS
    assert T == 4 and Q == 8 and HW == Q * CHUNK and CHUNK == J * BLOCK and B % 2 == 0
    assert NBN * BN_CHUNK == HW

    x_tiles = x.rearrange("b (t p) h w -> b p t (h w)", p=P)
    out_tiles = out.rearrange("b (t p) h w -> b p t (h w)", p=P)

    with ExitStack() as ctx:
        def sb(name, shape, dt=F32):
            return ctx.enter_context(nc.sbuf_tensor(name, shape, dt))

        def ps(name, shape):
            return ctx.enter_context(nc.psum_tensor(name, shape, F32))

        def sem(name):
            return ctx.enter_context(nc.semaphore(name))

        xs = sb("xs", [P, 2, T, HW])
        rs = sb("rs", [P, SHARED + 2 * TA, HW])
        mx = sb("mx", [P, HW])
        wt = sb("wt", [P, 2, T, C])
        ident = sb("ident", [P, P])
        group_avg = sb("group_avg", [P, P])
        group_avg_part = sb("group_avg_part", [P, 2, P])
        chan_avg = sb("chan_avg", [P, 32])
        ones = sb("ones", [P, 1])
        row_pick = sb("row_pick", [P, 4])
        part_pick = sb("part_pick", [P, 2])
        ident_bf = sb("ident_bf", [P, P], BF16)
        cmean_rows = sb("cmean_rows", [P, BANKS, CHUNK])
        control_sb = cmean_rows[:, :, :].rearrange("p b f -> p (b f)")[:, 0:C]
        half_neg = sb("half_neg", [P, T])
        bnst = sb("bnst", [P, 2, NBN, 6])
        bnag = sb("bnag", [P, 2, 2])
        bnsq = sb("bnsq", [P, 2])
        st = sb("st", [P, 2, T])
        st_dve = sb("st_dve", [P, 2, 2])
        square_rest = sb("square_rest", [P, 1])
        mean_last = sb("mean_last", [P, 1])
        gst = sb("gst", [P, 2, T])
        gsq = sb("gsq", [P, T])
        gvar = sb("gvar", [P, T])
        geps = sb("geps", [P, T])
        rstd = sb("rstd", [P, T])
        mrs = sb("mrs", [P, T])
        shift = sb("shift", [P, T])
        rsum = sb("rsum", [P, T])
        peak = sb("peak", [P, T])
        margin = sb("margin", [P, T])
        fails = sb("fails", [P, T])
        flag = sb("flag", [1, 1], I32)
        fpeak = sb("fpeak", [P, T])
        fmargin = sb("fmargin", [P, T])
        keep = sb("keep", [P, T])
        cmax = sb("cmax", [P, NBLK])
        diff = sb("diff", [P, NBLK])
        negdiff = sb("negdiff", [P, NBLK])
        expd = sb("expd", [P, NBLK])
        bb = sb("bb", [P, NBLK])
        bb_rest = sb("bb_rest", [P, NBLK])
        bb_parts = sb("bb_parts", [P, 3, NBLK], BF16)
        ymax_parts = sb("ymax_parts", [P, T, NG])
        ymax = sb("ymax", [P, T])
        pooled = sb("pooled", [P, T, NG])
        logits = sb("logits", [P, 2 * T])
        exp_neg = sb("exp_neg", [P, T])
        den = sb("den", [P, T])
        control1 = sb("control1", [P, T])
        c3_high = sb("c3_high", [P, T])
        c3_low = sb("c3_low", [P, T])
        control3 = sb("control3", [P, T])
        control = sb("control", [P, T])
        thres = sb("thres", [P, T])

        ps_pix = ps("ps_pix", [P, 4, 512])
        ps_rows = ps("ps_rows", [P, BANKS, 512])
        ps_small = ps("ps_small", [P, 512])
        ps_group = ps("ps_group", [P, 512])
        group_sums_of = ps_group[:, 0:2 * T].rearrange("p (a t) -> p a t", t=T)
        ps_cols = ps_small[0:BLOCK, 0:NBLK]
        ps_control = ps_small[:, 64:64 + 2 * T].rearrange("p (m t) -> p m t", t=T)
        ps_logits = ps_small[:, 64:64 + 2 * T]
        ps_count = ps_small[0:1, 128:129]

        def turn_banks(part):
            return (ps_pix[:, 0:2, :], ps_pix[:, 2:4, :], ps_rows[:, :, :], ps_pix[:, 0:2, :])[part]

        x_loaded = [[[sem(f"x_loaded_{p}_{t}_{h}") for h in range(2)] for t in range(T)] for p in range(2)]
        x_stored = [[[sem(f"x_stored_{p}_{t}_{h}") for h in range(2)] for t in range(T)] for p in range(2)]
        w_loaded = [sem("w1_loaded"), sem("w3_loaded")]
        settled = {e: sem(f"settled_{n}") for n, e in
                   (("pe", nc.tensor), ("dve", nc.vector), ("pool", nc.gpsimd), ("sp", nc.sync))}
        const_step = sem("const_step")
        const_step_pool = sem("const_step_pool")
        mrs_ready = sem("mrs_ready")
        consts_ready = sem("consts_ready")
        ones_ready = sem("ones_ready")
        w_turned = sem("w_turned")
        wt_ready = sem("wt_ready")
        act_step = sem("act_step")
        stats_act = sem("stats_act")
        bn_done = sem("bn_done")
        bn_aggregated = sem("bn_aggregated")
        bn_squared = sem("bn_squared")
        stats_dve = sem("stats_dve")
        group_sums = sem("group_sums")
        group_copied = sem("group_copied")
        pool_step = sem("pool_step")
        affine_ready = sem("affine_ready")
        relu_done = sem("relu_done")
        fails_ready = sem("fails_ready")
        count_ready = sem("count_ready")
        flag_ready = sem("flag_ready")
        mask_step = sem("mask_step")
        r_final = sem("r_final")
        rows_tried = sem("rows_tried")
        rows_final = sem("rows_final")
        rows_copied = sem("rows_copied")
        cols_ready = sem("cols_ready")
        max_part = sem("max_part")
        max_tried = sem("max_tried")
        turned_tried = sem("turned_tried")
        turned = sem("turned")
        cmax_part = sem("cmax_part")
        negdiff_ready = sem("negdiff_ready")
        expd_ready = sem("expd_ready")
        bb_ready = sem("bb_ready")
        bb_rows = sem("bb_rows")
        gated = sem("gated")
        pooled_ready = sem("pooled_ready")
        control_rows = sem("control_rows")
        control_copied = sem("control_copied")
        control_ready = sem("control_ready")
        logits_ready = sem("logits_ready")
        exp_neg_ready = sem("exp_neg_ready")
        dve_step = sem("dve_step")
        kept = sem("kept")
        added = sem("added")
        added_last = sem("added_last")

        def slot(parity, t):
            return t if t < SHARED else SHARED + TA * parity + (t - SHARED)

        def r_tile(s, t):
            return rs[:, slot(s.parity, t), :]

        ADD_CREDIT = 2 * 2 * T

        def wait_r_slot_free(eng, s, t):
            before = 1 if t < SHARED else 2
            eng.wait_ge(added, s.count(2 * T, ADD_CREDIT - 2 * T * before + 2 * (t + 1)))

        LAST_SPLIT = 2

        def wait_added(eng, s, t, h, is_last):
            if is_last and t >= LAST_SPLIT:
                eng.wait_ge(added_last, 2 * (t - LAST_SPLIT) + h + 1)
            else:
                eng.wait_ge(added, s.count(2 * T, ADD_CREDIT + 2 * t + h + 1))

        def add_half(eng, s, t, h):
            cols = slice(HALF * h, HALF * (h + 1))
            xt = xs[:, s.parity, t, cols]
            return eng.tensor_tensor(xt, xt, r_tile(s, t)[:, cols], ALU.add)

        STATS_DVE = [1, 2]
        STATS_ACT = [0, 3]
        RELU_ORDER = [1, 2, 3, 0]
        ACT_STEPS = 8

        def wait_loaded(eng, s, t, h):
            eng.wait_ge(x_loaded[s.parity][t][h], s.slot_count(1))

        def each_sample(eng, body):
            with eng.Fori(0, B // 2 - 1) as i:
                for parity in range(2):
                    body(Sample(i, parity), True, True)
            for parity in range(2):
                body(Sample(B // 2 - 1, parity), parity == 0, False)

        def settle(eng):
            eng.sem_inc(settled[eng], 1)

        block = ctx.enter_context(nc.Block())

        @block.sync
        def _(sp):
            def dram_half(tiles, s, t, h):
                return tiles[bass.ds(s.i * 2 + s.parity, 1), :, t, HALF * h:HALF * (h + 1)
                             ].rearrange("b p f -> (b p) f")

            def load(s, t, h):
                sp.dma_start(xs[:, s.parity, t, HALF * h:HALF * (h + 1)], dram_half(x_tiles, s, t, h)
                             ).then_inc(x_loaded[s.parity][t][h], 16)

            def store(s, t, h, is_last):
                wait_added(sp, s, t, h, is_last)
                settle(sp)
                sp.dma_start(dram_half(out_tiles, s, t, h), xs[:, s.parity, t, HALF * h:HALF * (h + 1)]
                             ).then_inc(x_stored[s.parity][t][h], 16)

            for t in STATS_ACT + STATS_DVE:
                for h in range(2):
                    load(Sample(0, 0), t, h)
            for m, w in enumerate((w1, w3)):
                sp.dma_start(rs[:, slot(1, SHARED + m), 0:T * C].rearrange("p (k c) -> p k c", k=T),
                             w.rearrange("(k p) c -> p k c", p=P)).then_inc(w_loaded[m], 16)
            for t in range(T):
                for h in range(2):
                    load(Sample(0, 1), t, h)

            def reload(s, t, h):
                sp.wait_ge(x_stored[s.parity][t][h], s.slot_count(1))
                settle(sp)
                load(Sample(s.i + 1, s.parity), t, h)

            def sample(s, has_next, has_second_next):
                halves = [(t, h) for t in range(T) for h in range(2)]
                for n, (t, h) in enumerate(halves):
                    store(s, t, h, not has_next)
                    if has_second_next:
                        for m in RELOADS_AFTER[n]:
                            reload(s, *halves[m])

            each_sample(sp, sample)
            for parity in range(2):
                for t in range(T):
                    for h in range(2):
                        sp.wait_ge(x_stored[parity][t][h], 16 * (B // 2))

        @block.tensor
        def _(pe):
            def channel_mean_tile(s, t, last_sem):
                for q in range(Q):
                    b, k = q // 4, q % 4
                    mm = pe.matmul(ps_rows[32 * k:32 * k + 32, b, 0:CHUNK], chan_avg[:, :],
                                   r_tile(s, t)[:, CHUNK * q:CHUNK * (q + 1)],
                                   start=(t == RELU_ORDER[0]), stop=(t == RELU_ORDER[-1]), skip_group_check=True,
                                   tile_position=(0, 32 * k))
                if last_sem is not None:
                    mm.then_inc(last_sem, 1)

            order = RELU_ORDER

            def group_stats(s):
                last = STATS_ACT[1]
                pe.wait_ge(act_step, s.count(ACT_STEPS, ACT_STEPS - 1))
                pe.matmul(group_sums_of[:, :, 0:last], group_avg[:, :], st[:, :, 0:last],
                          start=True, stop=False, skip_group_check=True)
                pe.wait_ge(stats_dve, s.count(1, 1))
                for u, t in enumerate(STATS_DVE):
                    mm = pe.matmul(group_sums_of[:, :, t], group_avg_part[:, u, :], st_dve[:, :, u],
                                   start=False, stop=(u == 1), skip_group_check=True)
                mm.then_inc(group_sums, 1)
                pe.wait_ge(act_step, s.count(ACT_STEPS, ACT_STEPS))
                pe.wait_ge(group_copied, s.count(2, 1))
                pe.matmul(group_sums_of[:, 0, last:last + 1], group_avg[:, :], mean_last[:, :],
                          start=True, stop=True, skip_group_check=True)
                pe.matmul(group_sums_of[:, 1, last:last + 1], group_avg[:, :], st[:, 1, last:last + 1],
                          start=True, stop=False, skip_group_check=True)
                pe.wait_ge(stats_act, s.count(1, 1))
                pe.matmul(group_sums_of[:, 1, last:last + 1], group_avg[:, :], square_rest[:, :],
                          start=False, stop=True, skip_group_check=True).then_inc(group_sums, 1)

            def channel_mean_first(s):
                for n, t in enumerate(order[:-1]):
                    pe.wait_ge(relu_done, s.count(T, n + 1))
                    channel_mean_tile(s, t, None)

            pe.wait_ge(consts_ready, 1)
            pe.wait_ge(ones_ready, 1)
            group_stats(Sample(0, 0))
            for m in range(2):
                pe.wait_ge(w_loaded[m], 16)
                for k in range(T):
                    n = T * m + k
                    if n >= 4:
                        pe.wait_ge(wt_ready, n - 3)
                    for c in range(T):
                        mm = pe.transpose(ps_pix[:, n % 4, P * c:P * (c + 1)],
                                          rs[:, slot(1, SHARED + m), C * c + P * k:C * c + P * (k + 1)],
                                          ident[:, :])
                    mm.then_inc(w_turned, 1)
            channel_mean_first(Sample(0, 0))

            def keep_clock(n):
                for _ in range(n):
                    pe.matmul(ps_group[:, 256:512], ident[:, :], wt[:, 0, 0, 0:256], start=True, stop=True,
                              skip_group_check=True)

            def sample(s, has_next, _):
                pe.wait_ge(relu_done, s.count(T, T))
                channel_mean_tile(s, order[-1], rows_tried)
                pe.wait_ge(group_copied, s.count(2, 2))
                keep_clock(3)
                pe.wait_ge(fails_ready, s.count(1, 1))
                for t in range(T):
                    mm = pe.matmul(ps_count, fails[:, t:t + 1], ones[:, :], start=(t == 0), stop=(t == T - 1))
                mm.then_inc(count_ready, 1)

                def turn(part, done):
                    for n in range(8):
                        blk = 8 * part + n
                        mm = pe.transpose(turn_banks(part)[0:BLOCK, n // 4, P * (n % 4):P * (n % 4 + 1)],
                                          mx[:, BLOCK * blk:BLOCK * (blk + 1)], ident[:, :])
                    if done is not None:
                        mm.then_inc(done, 1)

                for part in range(2):
                    pe.wait_ge(max_tried, s.count(2, part + 1))
                    turn(part, turned_tried)
                keep_clock(2)
                pe.wait_ge(flag_ready, s.count(1, 1))
                settle(pe)
                open_channels = pe.value_load(flag[0:1, 0:1], min_val=0, max_val=C)
                with pe.If(open_channels > 0):
                    pe.wait_ge(r_final, s.count(1, 1))
                    for t in order:
                        channel_mean_tile(s, t, None)
                    turn(0, None)
                    turn(1, rows_final)
                with pe.Else():
                    pe.sem_inc(rows_final, 1)
                pe.wait_ge(rows_copied, s.count(1, 1))
                pe.wait_ge(max_part, s.count(2, 1))
                turn(2, turned)
                for b in range(BANKS):
                    for j in range(J):
                        first = 4 * J * b + j
                        mm = pe.matmul(ps_cols[:, first:first + 3 * J + 1:J],
                                       cmean_rows[:, b, BLOCK * j:BLOCK * (j + 1)], row_pick[:, :],
                                       start=True, stop=True)
                mm.then_inc(cols_ready, 1)

                pe.wait_ge(cmax_part, s.count(4, 1))
                pe.wait_ge(max_part, s.count(2, 2))
                turn(3, turned)

                keep_clock(5)
                pe.wait_ge(bb_ready, s.count(1, 1))
                for g in range(NG):
                    if g >= 2:
                        pe.wait_ge(gated, s.count(NG * T, T * (g - 1)))
                    for n in range(GC * J):
                        blk = GC * J * g + n
                        for part in range(3):
                            mm = pe.matmul(ps_pix[:, 2 * (g % 2) + n // J, BLOCK * (n % J):BLOCK * (n % J + 1)],
                                           bb_parts[0:BLOCK, part, blk:blk + 1].to_broadcast([BLOCK, P]),
                                           ident_bf[0:BLOCK, 0:BLOCK], start=(part == 0), stop=(part == 2))
                    mm.then_inc(bb_rows, 1)
                    keep_clock([0, 2, 2, 2][g])

                pe.wait_ge(gated, s.count(NG * T, (NG - 1) * T))
                keep_clock(3)

                for k in range(T):
                    pe.wait_ge(pooled_ready, s.count(T, k + 1))
                    for m in range(2):
                        first = 32 * (m + 2 * (k % 2))
                        mm = pe.matmul(ps_rows[first:first + NG, 0, :], pooled[:, k, :], wt[:, m, k, :],
                                       start=(k < 2), stop=(k >= T - 2), skip_group_check=True,
                                       tile_position=(0, first))
                mm.then_inc(control_rows, 1)
                pe.wait_ge(control_copied, s.count(1, 1))
                for c in range(T):
                    mm = pe.matmul(ps_control[:, :, c], control_sb[:, P * c:P * (c + 1)], part_pick[:, :],
                                   start=True, stop=True)
                mm.then_inc(control_ready, 1)

                if has_next:
                    group_stats(s.next())
                    channel_mean_first(s.next())

            each_sample(pe, sample)

        @block.scalar
        def _(act):
            def moment(s, t, cols, func, scale, total):
                return act.activation(r_tile(s, max(t, SHARED))[:, cols], xs[:, s.parity, t, cols], func,
                                      scale=scale, accum_out=total)

            def square(s, t, cols, total):
                return moment(s, t, cols, ACT.Square, float(HW) ** -0.5, total)

            def mean(s, t, cols, total):
                return moment(s, t, cols, ACT.Identity, 1.0 / HW, total)

            def stats_early(s):
                steps = Steps(act, act_step, s, ACT_STEPS)
                wait_r_slot_free(act, s, SHARED)
                for h in range(2):
                    wait_loaded(act, s, STATS_ACT[0], h)
                steps.step(square(s, STATS_ACT[0], slice(0, HW), st[:, 1, STATS_ACT[0]:STATS_ACT[0] + 1]))
                steps.wait()
                steps.step(mean(s, STATS_ACT[0], slice(0, HW), st[:, 0, STATS_ACT[0]:STATS_ACT[0] + 1]))
                return steps

            def stats_rest(s, steps, u):
                t, cols = STATS_DVE[u], slice(BN_PIXELS[u], HW)
                wait_loaded(act, s, t, 1)
                wait_r_slot_free(act, s, t)
                steps.wait()
                steps.step(square(s, t, cols, st[:, 1, t:t + 1]))
                steps.wait()
                steps.step(mean(s, t, cols, st[:, 0, t:t + 1]))

            def stats_last_first(s, steps):
                t = STATS_ACT[1]
                wait_r_slot_free(act, s, t)
                wait_loaded(act, s, t, 0)
                steps.step(square(s, t, slice(0, HALF), st[:, 1, t:t + 1]))

            def stats_last_rest(s, steps):
                t = STATS_ACT[1]
                wait_loaded(act, s, t, 1)
                steps.wait()
                steps.step(mean(s, t, slice(0, HW), mean_last[:, :]))
                assert steps.done == ACT_STEPS
                copy_group(s, 0)
                steps.wait()
                square(s, t, slice(HALF, HW), square_rest[:, :]).then_inc(stats_act, 1)
                copy_group(s, 1)

            def copy_group(s, part):
                c = slice(0, STATS_ACT[1]) if part == 0 else slice(STATS_ACT[1], T)
                act.wait_ge(group_sums, s.count(2, part + 1))
                act.activation(gst[:, :, c], group_sums_of[:, :, c], ACT.Identity).then_inc(group_copied, 1)

            def relu(s):
                for t in RELU_ORDER:
                    act.wait_ge(affine_ready, s.count(2, 1 if t < STATS_ACT[1] else 2))
                    if t != STATS_ACT[1]:
                        wait_r_slot_free(act, s, t)
                    act.activation(r_tile(s, t), xs[:, s.parity, t, :], ACT.Relu, bias=shift[:, t:t + 1],
                                   scale=rstd[:, t:t + 1], accum_out=rsum[:, t:t + 1]).then_inc(relu_done, 1)

            act.wait_ge(ones_ready, 1)
            first = Sample(0, 0)
            steps = stats_early(first)
            stats_last_first(first, steps)
            for u in range(2):
                stats_rest(first, steps, u)
            stats_last_rest(first, steps)
            relu(Sample(0, 0))
            act.wait_ge(wt_ready, 2 * T)

            def sample(s, has_next, _):
                act.wait_ge(rows_tried, s.count(1, 1))
                act.wait_ge(rows_final, s.count(1, 1))
                act.activation(cmean_rows[:, :, :], ps_rows[:, :, 0:CHUNK], ACT.Identity).then_inc(rows_copied, 1)
                if has_next:
                    steps = stats_early(s.next())
                act.wait_ge(negdiff_ready, s.count(1, 1))
                act.activation(expd[0:BLOCK, :], negdiff[0:BLOCK, :], ACT.Exp).then_inc(expd_ready, 1)
                if has_next:
                    stats_rest(s.next(), steps, 0)
                for g in range(NG):
                    for t in range(T):
                        act.wait_ge(gated, s.count(NG * T, T * g + t + 1))
                        y = r_tile(s, t)[:, GPIX * g:GPIX * (g + 1)]
                        ins = act.activation(y, y, ACT.Identity, accum_out=pooled[:, t, g:g + 1])
                        if g == NG - 1:
                            ins.then_inc(pooled_ready, 1)
                act.wait_ge(control_rows, s.count(1, 1))
                act.activation(control_sb, ps_rows[:, 0, :], ACT.Identity).then_inc(control_copied, 1)
                if has_next:
                    stats_last_first(s.next(), steps)
                act.wait_ge(logits_ready, s.count(1, 1))
                act.activation(exp_neg[:, :], logits[:, 0:T], ACT.Exp, scale=-1.0).then_inc(exp_neg_ready, 1)
                if has_next:
                    stats_rest(s.next(), steps, 1)
                    stats_last_rest(s.next(), steps)
                    relu(s.next())

            each_sample(act, sample)

        @block.vector
        def _(dve):
            MASK_STEPS = 9
            DVE_STEPS = 16

            dve.memset(chan_avg[:, :], 1.0 / C)
            dve.memset(ps_rows[:, 0, :], 0.0)
            dve.memset(st[:, :, :], 0.0)
            dve.memset(half_neg[:, :], -0.5)
            dve.memset(ones[:, :], 1.0).then_inc(ones_ready, 1)

            def stats_part(s, n):
                chunks = [(u, c) for u in range(2) for c in range(BN_CHUNKS[u])]
                cut = [0, 1, 4, len(chunks) - 1, len(chunks)]
                for u, c in chunks[cut[n]:cut[n + 1]]:
                    t = STATS_DVE[u]
                    if c == 0:
                        wait_loaded(dve, s, t, 0)
                    if c == HALF // BN_CHUNK:
                        wait_loaded(dve, s, t, 1)
                    ins = dve.bn_stats(bnst[:, u, c, :], xs[:, s.parity, t, BN_CHUNK * c:BN_CHUNK * (c + 1)])
                return ins

            def stats_aggregate(s):
                dve.wait_ge(bn_done, s.count(1, 1))
                settle(dve)
                for u in range(2):
                    ins = dve.bn_aggr(bnag[:, u, :], bnst[:, u, 0:BN_CHUNKS[u], :].rearrange("p c s -> p (c s)"))
                ins.then_inc(bn_aggregated, 1)

            def stats_moments(s):
                dve.wait_ge(bn_aggregated, s.count(1, 1))
                dve.tensor_copy(st_dve[:, 0, :], bnag[:, :, 0])
                dve.tensor_tensor(bnsq[:, :], bnag[:, :, 0], bnag[:, :, 0], ALU.mult).then_inc(bn_squared, 1)

            def stats_mean_square(s):
                dve.wait_ge(bn_squared, s.count(1, 1))
                dve.tensor_tensor(st_dve[:, 1, :], bnsq[:, :], bnag[:, :, 1], ALU.add
                                  ).then_inc(stats_dve, 1)

            first = Sample(0, 0)
            for n in range(4):
                ins = stats_part(first, n)
            ins.then_inc(bn_done, 1)
            stats_aggregate(first)
            stats_moments(first)
            stats_mean_square(first)
            for n in range(2 * T):
                dve.wait_ge(w_turned, n + 1)
                dve.tensor_copy(wt[:, n // T, n % T, :], ps_pix[:, n % 4, :]).then_inc(wt_ready, 1)

            def mask_channels(s):
                masks = Steps(dve, mask_step, s, MASK_STEPS)
                dve.wait_ge(rows_tried, s.count(1, 1))
                dve.wait_ge(turned_tried, s.count(2, 2))
                for t in range(T):
                    ins = dve.tensor_reduce(fpeak[:, t:t + 1], r_tile(s, t), AX.X, ALU.max)
                masks.step(ins)
                masks.wait()
                masks.step(dve.scalar_tensor_tensor(fmargin[:, :], rsum[:, :], -1.0 / HW, fpeak[:, :],
                                                    ALU.mult, ALU.add))
                masks.wait()
                masks.step(dve.tensor_scalar(keep[:, :], fmargin[:, :], PEAK_MARGIN, None, ALU.is_ge))
                masks.wait()
                for t in range(T):
                    ins = dve.tensor_scalar(r_tile(s, t), r_tile(s, t), keep[:, t:t + 1], None, ALU.mult)
                masks.step(ins)
                masks.wait()
                return masks

            def sample(s, has_next, _):
                steps = Steps(dve, dve_step, s, DVE_STEPS)
                nxt = s.next() if has_next else None

                def max_step(n, h):
                    cols = slice(HALF * h, HALF * (h + 1))
                    prev = r_tile(s, RELU_ORDER[0]) if n == 0 else mx[:, :]
                    return dve.tensor_tensor(mx[:, cols], prev[:, cols], r_tile(s, RELU_ORDER[n + 1])[:, cols],
                                             ALU.max)

                def max_last(part):
                    cols = slice(GPIX * part, GPIX * (part + 1))
                    return dve.tensor_tensor(mx[:, cols], mx[:, cols], r_tile(s, RELU_ORDER[T - 1])[:, cols],
                                             ALU.max)

                dve.wait_ge(relu_done, s.count(T, 2))
                steps.step(max_step(0, 0))
                steps.step(max_step(0, 1))
                dve.wait_ge(relu_done, s.count(T, 3))
                steps.wait(back=1)
                steps.step(max_step(1, 0))
                dve.wait_ge(relu_done, s.count(T, T))
                a = slot(s.parity, SHARED)
                dve.tensor_reduce(peak[:, 0:SHARED], rs[:, 0:SHARED, 0:SUBSET], AX.X, ALU.max)
                steps.step(dve.tensor_reduce(peak[:, SHARED:T], rs[:, a:a + TA, 0:SUBSET], AX.X, ALU.max))
                steps.wait()
                steps.step(dve.scalar_tensor_tensor(margin[:, :], rsum[:, :], -1.0 / HW, peak[:, :],
                                                    ALU.mult, ALU.add))
                steps.wait(back=2)
                max_last(0).then_inc(max_tried, 1)
                steps.wait()
                dve.tensor_scalar(fails[:, :], margin[:, :], PEAK_MARGIN, None, ALU.is_lt
                                  ).then_inc(fails_ready, 1)
                max_last(1).then_inc(max_tried, 1)
                dve.wait_ge(count_ready, s.count(1, 1))
                dve.tensor_copy(flag[:, :], ps_count).then_inc(flag_ready, 1)
                steps.step(max_step(1, 1))
                dve.wait_ge(flag_ready, s.count(1, 1))
                settle(dve)
                open_channels = dve.value_load(flag[0:1, 0:1], min_val=0, max_val=C)
                with dve.If(open_channels > 0):
                    masks = mask_channels(s)
                    for n in range(2):
                        for h in range(2):
                            masks.wait()
                            masks.step(max_step(n, h))
                    masks.wait()
                    masks.step(max_last(0))
                    max_last(1).then_inc(r_final, 1)
                    assert masks.done == MASK_STEPS
                with dve.Else():
                    dve.sem_inc(mask_step, MASK_STEPS)
                    dve.sem_inc(r_final, 1)
                steps.wait()
                dve.wait_ge(r_final, s.count(1, 1))
                for part in range(2, 4):
                    max_last(part).then_inc(max_part, 1)
                for part in range(4):
                    if part < 2:
                        dve.wait_ge(turned_tried, s.count(2, part + 1))
                        dve.wait_ge(rows_final, s.count(1, 1))
                    else:
                        dve.wait_ge(turned, s.count(2, part - 1))
                    ins = dve.tensor_reduce(
                        cmax[0:BLOCK, 8 * part:8 * (part + 1)],
                        turn_banks(part)[0:BLOCK, :, :].rearrange("p b (n c) -> p (b n) c", c=P), AX.X, ALU.max)
                    ins.then_inc(cmax_part, 1)
                dve.wait_ge(cmax_part, s.count(4, 4))
                dve.wait_ge(cols_ready, s.count(1, 1))
                steps.step(dve.tensor_tensor(diff[0:BLOCK, :], cmax[0:BLOCK, :], ps_cols, ALU.subtract))
                steps.wait()
                dve.scalar_tensor_tensor(negdiff[0:BLOCK, :], diff[0:BLOCK, :], -1.0, diff[0:BLOCK, :],
                                         ALU.mult, ALU.min).then_inc(negdiff_ready, 1)
                if has_next:
                    stats_part(nxt, 0)
                dve.wait_ge(expd_ready, s.count(1, 1))
                def cols_of(a):
                    return a[0:BLOCK, :]

                dve.tensor_scalar(cols_of(bb), cols_of(expd), -1.0, 1.0, ALU.mult, ALU.add)
                steps.step(dve.tensor_scalar(bb_parts[0:BLOCK, 0, :], cols_of(expd), -1.0, 1.0,
                                             ALU.mult, ALU.add))
                steps.wait()
                dve.tensor_tensor(cols_of(bb_rest), cols_of(bb), bb_parts[0:BLOCK, 0, :], ALU.subtract)
                steps.step(dve.tensor_tensor(bb_parts[0:BLOCK, 1, :], cols_of(bb), bb_parts[0:BLOCK, 0, :],
                                             ALU.subtract))
                steps.wait()
                dve.tensor_tensor(bb_parts[0:BLOCK, 2, :], cols_of(bb_rest), bb_parts[0:BLOCK, 1, :],
                                  ALU.subtract).then_inc(bb_ready, 1)
                if has_next:
                    stats_part(nxt, 1)

                for g in range(NG):
                    dve.wait_ge(bb_rows, s.count(NG, g + 1))
                    settle(dve)
                    b = 2 * (g % 2)
                    for t in range(T):
                        y = r_tile(s, t)[:, GPIX * g:GPIX * (g + 1)].rearrange("p (b f) -> p b f", f=CHUNK)
                        dve.tensor_tensor_reduce(out=y, in0=y, in1=ps_pix[:, b:b + 2, 0:CHUNK], scale=1.0,
                                                 scalar=0.0, op0=ALU.mult, op1=ALU.max,
                                                 accum_out=ymax_parts[:, t, g:g + 1]).then_inc(gated, 1)
                dve.wait_ge(gated, s.count(NG * T, NG * T))
                steps.step(dve.tensor_reduce(ymax[:, :], ymax_parts[:, :, :], AX.X, ALU.max))
                if has_next:
                    stats_part(nxt, 2)
                dve.wait_ge(control_ready, s.count(1, 1))
                dve.tensor_scalar(logits[:, :], ps_logits, 1.0 / HW, None, ALU.mult).then_inc(logits_ready, 1)
                if has_next:
                    stats_part(nxt, 3).then_inc(bn_done, 1)
                dve.wait_ge(logits_ready, s.count(1, 1))
                dve.scalar_tensor_tensor(c3_high[:, :], logits[:, T:2 * T], CONTROL_FLOOR,
                                         logits[:, T:2 * T], ALU.is_ge, ALU.mult)
                steps.step(dve.tensor_scalar(c3_low[:, :], logits[:, T:2 * T], CONTROL_FLOOR, CONTROL_DEFAULT,
                                             ALU.is_lt, ALU.mult))
                steps.wait()
                steps.step(dve.tensor_tensor(control3[:, :], c3_high[:, :], c3_low[:, :], ALU.add))
                if has_next:
                    stats_aggregate(nxt)
                steps.wait()
                steps.step(dve.tensor_tensor(control[:, :], control3[:, :], ymax[:, :], ALU.mult))
                dve.wait_ge(exp_neg_ready, s.count(1, 1))
                steps.step(dve.tensor_scalar(den[:, :], exp_neg[:, :], 1.0, None, ALU.add))
                if has_next:
                    stats_moments(nxt)
                steps.wait()
                steps.step(dve.reciprocal(control1[:, :], den[:, :]))
                if has_next:
                    stats_mean_square(nxt)
                steps.wait()
                steps.step(dve.tensor_tensor(thres[:, :], control[:, :], control1[:, :], ALU.mult))
                steps.wait()

                def keep_tile(t):
                    r = r_tile(s, t)
                    return dve.scalar_tensor_tensor(r, r, thres[:, t:t + 1], r, ALU.is_ge, ALU.mult
                                                    ).then_inc(kept, 1)

                for t in range(T):
                    keep_tile(t)
                if not has_next:
                    for t in range(LAST_SPLIT, T):
                        dve.wait_ge(kept, s.count(T, t + 1))
                        for h in range(2):
                            add_half(dve, s, t, h).then_inc(added_last, 1)
                assert steps.done == DVE_STEPS, steps.done

            each_sample(dve, sample)

        @block.gpsimd
        def _(pool):
            POOL_STEPS = 4
            pool.memset(ident[:, :], 0.0)
            pool.memset(row_pick[:, :], 0.0)
            pool.memset(part_pick[:, :], 0.0)
            for u in range(2):
                pool.memset(group_avg_part[:, u, :], BN_PIXELS[u] / HW / PER_GROUP)
            pool.memset(group_avg[:, :], 1.0 / PER_GROUP).then_inc(const_step_pool, 1)
            pool.wait_ge(const_step_pool, 1)
            pool.affine_select(out=ident[:, :], in_=ident[:, :], compare_op=ALU.not_equal, fill=1.0, base=0,
                               pattern=[[-1, P]], channel_multiplier=1)
            pool.affine_select(out=row_pick[:, :], in_=row_pick[:, :], compare_op=ALU.not_equal, fill=1.0,
                               base=0, pattern=[[-32, 4]], channel_multiplier=1)
            group_blocks = [a.rearrange("p (g c) -> p g c", c=PER_GROUP)
                            for a in (group_avg[:, :], group_avg_part[:, 0, :], group_avg_part[:, 1, :])]
            for blocks in group_blocks:
                ins = pool.affine_select(out=blocks, in_=blocks, compare_op=ALU.is_ge, fill=0.0, base=0,
                                         pattern=[[-PER_GROUP, P // PER_GROUP], [0, PER_GROUP]],
                                         channel_multiplier=1)
            ins.then_inc(const_step_pool, 1)
            pool.wait_ge(const_step_pool, 2)
            for n in range(2 * NG):
                pool.affine_select(out=part_pick[:, :], in_=part_pick[:, :], compare_op=ALU.not_equal, fill=1.0,
                                   base=-(n % NG) - 64 * (n // NG), pattern=[[-32, 2]],
                                   channel_multiplier=1).then_inc(const_step_pool, 1)
                pool.wait_ge(const_step_pool, 3 + n)
            pool.tensor_copy(ident_bf[:, :], ident[:, :])
            for blocks in group_blocks:
                ins = pool.affine_select(out=blocks, in_=blocks, compare_op=ALU.is_ge, fill=0.0,
                                         base=PER_GROUP - 1,
                                         pattern=[[PER_GROUP, P // PER_GROUP], [0, PER_GROUP]],
                                         channel_multiplier=-1)
            ins.then_inc(consts_ready, 1)
            pool.sem_inc(added, ADD_CREDIT)
            pool.wait_ge(ones_ready, 1)

            def affine(s, part):
                steps = Steps(pool, pool_step, s, 2 * POOL_STEPS)
                steps.done = POOL_STEPS * part
                c = slice(0, STATS_ACT[1]) if part == 0 else slice(STATS_ACT[1], T)
                pool.wait_ge(group_copied, s.count(2, part + 1))
                steps.step(pool.tensor_tensor(gsq[:, c], gst[:, 0, c], gst[:, 0, c], ALU.mult))
                steps.wait()
                steps.step(pool.tensor_tensor(gvar[:, c], gst[:, 1, c], gsq[:, c], ALU.subtract))
                steps.wait()
                settle(pool)
                steps.step(pool.tensor_scalar(geps[:, c], gvar[:, c], 0.0, GN_EPS, ALU.max, ALU.add))
                steps.wait()
                steps.step(pool.tensor_tensor(rstd[:, c], geps[:, c], half_neg[:, c], ALU.pow))
                steps.wait()
                pool.tensor_tensor(mrs[:, c], gst[:, 0, c], rstd[:, c], ALU.mult).then_inc(mrs_ready, 1)
                pool.wait_ge(mrs_ready, s.count(2, part + 1))
                settle(pool)
                pool.tensor_scalar(shift[:, c], mrs[:, c], -1.0, 1.0, ALU.mult, ALU.mult
                                   ).then_inc(affine_ready, 1)
                assert steps.done == POOL_STEPS * (part + 1)

            for part in range(2):
                affine(Sample(0, 0), part)

            def sample(s, has_next, _):
                if has_next:
                    affine(s.next(), 0)
                for t in range(T if has_next else LAST_SPLIT):
                    pool.wait_ge(kept, s.count(T, t + 1))
                    for h in range(2):
                        add_half(pool, s, t, h).then_inc(added, 1)
                        if has_next and (t, h) == (0, 0):
                            affine(s.next(), 1)

            each_sample(pool, sample)


_INS = ["x", "L0_conv_W1", "L0_conv_W3"]


def kernel(**inputs):
    import numpy as np
    import concourse.bacc as bacc
    from concourse.bass_utils import run_bass_kernel_spmd

    nc = bacc.Bacc("TRN2", target_bir_lowering=False, num_devices=1, dynamic_dma_scratch_size=1024)
    arrays, args = {}, []
    for name in _INS:
        a = np.ascontiguousarray(inputs[name])
        arrays[f"in_{name}"] = a
        args.append(nc.dram_tensor(f"in_{name}", a.shape, mybir.dt.from_np(a.dtype), kind="ExternalInput").ap())
    shape = inputs["x"].shape
    args.append(nc.dram_tensor("out_0", shape, F32, kind="ExternalOutput").ap())
    gated_sparsifier(nc, *args)
    r = run_bass_kernel_spmd(nc, [arrays], core_ids=[0])
    return r.results[0]["out_0"]
```
